# Optimizing a Trainium2 kernel written in Bass

```python
import numpy as np
import jax
import jax.numpy as jnp

def _softmax(x, axis=-1):
    return jax.nn.softmax(x, axis=axis)

def _gelu(x):
    return jax.nn.gelu(x, approximate=True)

def _silu(x):
    return jax.nn.silu(x)

def _sigmoid(x):
    return jax.nn.sigmoid(x)

def _layernorm(x, axis=-1, eps=1e-05):
    m = jnp.mean(x, axis=axis, keepdims=True)
    v = jnp.var(x, axis=axis, keepdims=True)
    return (x - m) / jnp.sqrt(v + eps)

def _scatter_add(tgt, idx, src, axis=0):
    return tgt.at[idx].add(src)

def _segment_sum(src, seg, n):
    return jax.ops.segment_sum(src, seg, n)
kernel_name = 'mk_xattn_ffn_d1_seqx_r4_6010e0'

def setup_inputs(seed: int=0):
    np.random.seed(seed)
    _w = jnp.asarray

    def _rec_inputs():
        import jax
        import jax.numpy as jnp
        _rk = jax.random.key(seed)
        x = -0.0003929 + 0.9999 * jax.random.normal(jax.random.fold_in(_rk, 1), (4, 512, 512), jnp.float32)
        _lenS = 512 - jax.random.randint(jax.random.fold_in(_rk, 7), (4,), 0, max(1, 512 // 4) + 1, jnp.int32)
        _lenS2 = 1601 - jax.random.randint(jax.random.fold_in(_rk, 8), (4,), 0, max(1, 1601 // 4) + 1, jnp.int32)
        _ctx_2048P = jax.random.normal(jax.random.fold_in(_rk, 11), (4, 16, 512), jnp.float32)
        _ctx_2048c = jax.random.dirichlet(jax.random.fold_in(_rk, 511), 0.3 * jnp.ones((16,), jnp.float32), (4, 1601))
        _ctx_2048t = jnp.einsum('bsk,bkd->bsd', _ctx_2048c, _ctx_2048P)
        _ctx_2048t = _ctx_2048t * jax.lax.rsqrt(jnp.mean(jnp.square(_ctx_2048t)) + 1e-12) * 0.953939
        ctx_2048 = -0.000514642 + 1.00011 * (_ctx_2048t + 0.3 * jax.random.normal(jax.random.fold_in(_rk, 611), (4, 1601, 512), jnp.float32))
        _validS = jnp.arange(512)[None, :] < _lenS[:, None]
        _validS2 = jnp.arange(1601)[None, :] < _lenS2[:, None]
        _causal = jnp.tril(jnp.ones((512, 512), dtype=bool))
        mask_BxS2_ik0 = jnp.where(jnp.broadcast_to(_validS2[:, :], (4, 1601)), 0, 1).astype(jnp.int32)
        return (x, ctx_2048, mask_BxS2_ik0)
    x, ctx_2048, mask_BxS2_ik0 = _rec_inputs()

    def _L0_xattn_setup():
        import jax, jax.numpy as jnp
        import numpy as np
        import math
        H = 512
        NH = 16
        HD = H // NH
        EPS_LN = 1e-05
        RES_SCALE_MAX = 0.3

        def _nan_clean(x, lim=10000.0):
            return jnp.nan_to_num(x, nan=0.0, posinf=lim, neginf=-lim)
        key = jax.random.key(seed)
        ks = jax.random.split(key, 12)
        B, S, T = (4, 512, 64)
        std = 1.0 / math.sqrt(H)
        return {'hidden_states': jax.random.normal(ks[0], (B, S, H), jnp.float32), 'audio_tokens': jax.random.normal(ks[1], (B, T, H), jnp.float32), 'attention_mask': jax.random.randint(ks[2], (B, T), 0, 2, jnp.int32), 'Wq': jax.random.normal(ks[3], (H, H), jnp.float32) * std, 'bq': jnp.zeros((H,), jnp.float32), 'Wk': jax.random.normal(ks[4], (H, H), jnp.float32) * std, 'bk': jnp.zeros((H,), jnp.float32), 'Wv': jax.random.normal(ks[5], (H, H), jnp.float32) * std, 'bv': jnp.zeros((H,), jnp.float32), 'Wo': jax.random.normal(ks[6], (H, H), jnp.float32) * std, 'bo': jnp.zeros((H,), jnp.float32), 'ln_gamma': jnp.ones((H,), jnp.float32), 'ln_beta': jnp.zeros((H,), jnp.float32), 'residual_scale': jnp.float32(0.05)}
    _L0_xattn_all = _L0_xattn_setup()
    _L0_xattn_in = {k: v for k, v in _L0_xattn_all.items() if k in ('Wq', 'bq', 'Wk', 'bk', 'Wv', 'bv', 'Wo', 'bo', 'ln_gamma', 'ln_beta', 'residual_scale')}
    del _L0_xattn_all

    def _L0_ffn_setup():
        import jax, jax.numpy as jnp
        import numpy as np
        HIDDEN = 512
        INTER = 2048
        SCALE = 64.0

        def fwht(x):
            orig_shape = x.shape
            n = orig_shape[-1]
            x = x.reshape(-1, n)
            h = 1
            while h < n:
                x = x.reshape(-1, n // (2 * h), 2, h)
                a, b = (x[:, :, 0, :], x[:, :, 1, :])
                x = jnp.stack([a + b, a - b], axis=2).reshape(-1, n)
                h *= 2
            return (x / jnp.sqrt(jnp.asarray(n, x.dtype))).reshape(orig_shape)
        key = jax.random.key(seed)
        ks = jax.random.split(key, 8)
        inp = jax.random.normal(ks[0], (4, 512, HIDDEN), dtype=jnp.float32)
        SU_ug = jnp.where(jax.random.bernoulli(ks[1], 0.5, (HIDDEN,)), 1.0, -1.0).astype(jnp.float32)
        SU_dp = jnp.where(jax.random.bernoulli(ks[2], 0.5, (INTER,)), 1.0, -1.0).astype(jnp.float32)
        Wscale_ug = jax.random.uniform(ks[3], (2 * INTER,), jnp.float32, 0.5, 1.5)
        Wscale_dp = jax.random.uniform(ks[4], (HIDDEN,), jnp.float32, 0.5, 1.5)
        W_up = jax.random.normal(ks[5], (INTER, HIDDEN), dtype=jnp.float32) * 0.02
        W_gate = jax.random.normal(ks[6], (INTER, HIDDEN), dtype=jnp.float32) * 0.02
        W_down = jax.random.normal(ks[7], (HIDDEN, INTER), dtype=jnp.float32) * 0.02
        return {'input': inp, 'SU_ug': SU_ug, 'SU_dp': SU_dp, 'Wscale_ug': Wscale_ug, 'Wscale_dp': Wscale_dp, 'W_up': W_up, 'W_gate': W_gate, 'W_down': W_down}
    _L0_ffn_all = _L0_ffn_setup()
    _L0_ffn_in = {k: v for k, v in _L0_ffn_all.items() if k in ('SU_ug', 'SU_dp', 'Wscale_ug', 'Wscale_dp', 'W_up', 'W_gate', 'W_down')}
    del _L0_ffn_all
    return {'x': x, 'ctx_2048': ctx_2048, 'mask_BxS2_ik0': mask_BxS2_ik0, 'L0_xattn_Wq': _L0_xattn_in['Wq'], 'L0_xattn_bq': _L0_xattn_in['bq'], 'L0_xattn_Wk': _L0_xattn_in['Wk'], 'L0_xattn_bk': _L0_xattn_in['bk'], 'L0_xattn_Wv': _L0_xattn_in['Wv'], 'L0_xattn_bv': _L0_xattn_in['bv'], 'L0_xattn_Wo': _L0_xattn_in['Wo'], 'L0_xattn_bo': _L0_xattn_in['bo'], 'L0_xattn_ln_gamma': _L0_xattn_in['ln_gamma'], 'L0_xattn_ln_beta': _L0_xattn_in['ln_beta'], 'L0_xattn_residual_scale': _L0_xattn_in['residual_scale'], 'L0_ffn_SU_ug': _L0_ffn_in['SU_ug'], 'L0_ffn_SU_dp': _L0_ffn_in['SU_dp'], 'L0_ffn_Wscale_ug': _L0_ffn_in['Wscale_ug'], 'L0_ffn_Wscale_dp': _L0_ffn_in['Wscale_dp'], 'L0_ffn_W_up': _L0_ffn_in['W_up'], 'L0_ffn_W_gate': _L0_ffn_in['W_gate'], 'L0_ffn_W_down': _L0_ffn_in['W_down']}

def reference(x, ctx_2048, mask_BxS2_ik0, L0_xattn_Wq, L0_xattn_bq, L0_xattn_Wk, L0_xattn_bk, L0_xattn_Wv, L0_xattn_bv, L0_xattn_Wo, L0_xattn_bo, L0_xattn_ln_gamma, L0_xattn_ln_beta, L0_xattn_residual_scale, L0_ffn_SU_ug, L0_ffn_SU_dp, L0_ffn_Wscale_ug, L0_ffn_Wscale_dp, L0_ffn_W_up, L0_ffn_W_gate, L0_ffn_W_down):
    import jax
    import jax.numpy as jnp

    def _L0_xattn_ref(hidden_states, audio_tokens, attention_mask, Wq, bq, Wk, bk, Wv, bv, Wo, bo, ln_gamma, ln_beta, residual_scale):
        import jax, jax.numpy as jnp
        import numpy as np
        import math
        H = 512
        NH = 16
        HD = H // NH
        EPS_LN = 1e-05
        RES_SCALE_MAX = 0.3

        def _nan_clean(x, lim=10000.0):
            return jnp.nan_to_num(x, nan=0.0, posinf=lim, neginf=-lim)
        B, S, _ = hidden_states.shape
        T = audio_tokens.shape[1]
        hs = _nan_clean(hidden_states).astype(jnp.float32)
        at = _nan_clean(audio_tokens).astype(jnp.float32)

        def proj(x, W, b, L):
            y = x @ W.T + b
            return y.reshape(B, L, NH, HD).transpose(0, 2, 1, 3)
        q = _nan_clean(proj(hs, Wq, bq, S))
        k = _nan_clean(proj(at, Wk, bk, T))
        v = _nan_clean(proj(at, Wv, bv, T))
        scale = max(math.sqrt(HD), 1e-08)
        scores = jnp.einsum('bhsd,bhtd->bhst', q, k) / scale
        scores = jnp.clip(scores, -50.0, 50.0)
        scores = jnp.nan_to_num(scores, nan=0.0, posinf=50.0, neginf=-50.0)
        attend = (attention_mask.astype(jnp.float32) > 0.5)[:, None, None, :]
        scores = jnp.where(attend, scores, -10000.0)
        scores = jnp.clip(scores, -50.0, 50.0)
        probs = jax.nn.softmax(scores, axis=-1)
        probs = jnp.nan_to_num(probs, nan=0.0, posinf=1.0, neginf=0.0)
        probs = probs / (probs.sum(axis=-1, keepdims=True) + 1e-08)
        ctx = jnp.einsum('bhst,bhtd->bhsd', probs, v)
        ctx = ctx.transpose(0, 2, 1, 3).reshape(B, S, H)
        delta = _nan_clean(ctx @ Wo.T + bo)
        rs = jnp.clip(residual_scale, 0.0, RES_SCALE_MAX)
        delta = rs * delta
        mu = delta.mean(axis=-1, keepdims=True)
        var = jnp.mean((delta - mu) ** 2, axis=-1, keepdims=True)
        delta = (delta - mu) / jnp.sqrt(var + EPS_LN) * ln_gamma + ln_beta
        return delta

    def _L0_ffn_ref(input, SU_ug, SU_dp, Wscale_ug, Wscale_dp, W_up, W_gate, W_down):
        import jax, jax.numpy as jnp
        import numpy as np
        HIDDEN = 512
        INTER = 2048
        SCALE = 64.0

        def fwht(x):
            orig_shape = x.shape
            n = orig_shape[-1]
            x = x.reshape(-1, n)
            h = 1
            while h < n:
                x = x.reshape(-1, n // (2 * h), 2, h)
                a, b = (x[:, :, 0, :], x[:, :, 1, :])
                x = jnp.stack([a + b, a - b], axis=2).reshape(-1, n)
                h *= 2
            return (x / jnp.sqrt(jnp.asarray(n, x.dtype))).reshape(orig_shape)
        n = SU_ug.shape[0]
        x = input.reshape(-1, n)
        x = fwht(x * SU_ug) / SCALE
        x_up = x @ W_up.T * (Wscale_ug[:INTER] * SCALE)
        x_gate = x @ W_gate.T * (Wscale_ug[INTER:] * SCALE)
        x = jax.nn.silu(x_gate) * x_up
        x = fwht(x * SU_dp) / SCALE
        x = x @ W_down.T * (Wscale_dp * SCALE)
        return x.reshape(input.shape)
    x = x + _L0_xattn_ref(_layernorm(x, axis=-1), ctx_2048, mask_BxS2_ik0, L0_xattn_Wq, L0_xattn_bq, L0_xattn_Wk, L0_xattn_bk, L0_xattn_Wv, L0_xattn_bv, L0_xattn_Wo, L0_xattn_bo, L0_xattn_ln_gamma, L0_xattn_ln_beta, L0_xattn_residual_scale)
    x = x + _L0_ffn_ref(_layernorm(x, axis=-1), L0_ffn_SU_ug, L0_ffn_SU_dp, L0_ffn_Wscale_ug, L0_ffn_Wscale_dp, L0_ffn_W_up, L0_ffn_W_gate, L0_ffn_W_down)
    return x

_drawn_inputs = setup_inputs


def setup_inputs(seed=0):
    import zlib

    import numpy as np

    out = dict(_drawn_inputs(seed))
    spreads = {'L0_xattn_bq': (0.0, 0.267),
     'L0_xattn_bk': (0.0, 0.8),
     'L0_xattn_bv': (0.0, 0.1),
     'L0_xattn_bo': (0.0, 0.1),
     'L0_xattn_ln_gamma': (1.0, 0.2),
     'L0_xattn_ln_beta': (0.0, 0.1)}
    factors = {'L0_ffn_Wscale_dp': 2.716}
    for name, (base, spread) in spreads.items():
        noise = np.random.default_rng([zlib.crc32(name.encode()), seed]).standard_normal(out[name].shape)
        drawn = base * np.exp(spread * noise) if base else spread * noise
        out[name] = jnp.asarray(drawn.astype(out[name].dtype))
    for name, factor in factors.items():
        out[name] = (out[name] * factor).astype(out[name].dtype)
    return out
```

```python
import numpy as np
import concourse.bass as bass
from concourse import mybir
from contextlib import ExitStack

F32 = mybir.dt.float32
F32R = mybir.dt.float32r
I32 = mybir.dt.int32
ALU = mybir.AluOpType
ACT = mybir.ActivationFunctionType

B, S, H, T = 4, 512, 512, 1601
NH = 16
HD = H // NH
INTER = 2048
P = 128
HC = H // P
ST = S // P
TT = -(-T // P)
TLAST = T - (TT - 1) * P
TE = T + T % 2
TP = TT * P
LOW = float(np.float32(np.exp(-50.0)))
HIGH = float(np.float32(np.exp(50.0)))
EPS = 1e-5
PAIRS = B * NH // 2


class Mem:

    def __init__(self, nc, stack, prefix):
        self.nc, self.stack, self.prefix = nc, stack, prefix

    def sb(self, name, shape, dt=F32):
        return self.stack.enter_context(self.nc.sbuf_tensor(f"{self.prefix}_{name}", shape, dt))

    def ps(self, name, shape, dt=F32):
        return self.stack.enter_context(self.nc.psum_tensor(f"{self.prefix}_{name}", shape, dt))

    def sem(self, name):
        return self.stack.enter_context(self.nc.semaphore(f"{self.prefix}_{name}"))

    def sems(self, name, n):
        return [self.sem(f"{name}{i}") for i in range(n)]


NORM_STEPS = ST + 11


def row_moments(nc, dve, src, src_wait, step, base, ve_done, root_done, call, m):
    v = nc.vector
    for j in range(ST):
        src_wait(j)
        v.bn_stats(m.stats[:, j], src[:, j]).then_inc(step, 1)
    st = m.stats[:].rearrange("p j (o k) -> p k o j", o=2)
    mean, m2 = st[:, 1], st[:, 2]
    dve.wait_ge(step, base + ST)
    v.tensor_tensor(m.mean[:], mean[:, 0], mean[:, 1], ALU.add).then_inc(step, 1)
    v.tensor_tensor(m.diff[:], mean[:, 0], mean[:, 1], ALU.subtract).then_inc(step, 1)
    v.tensor_tensor(m.ve[:], m2[:, 0], m2[:, 1], ALU.add).then_inc(step, 1)
    dve.wait_ge(step, base + ST + 3)
    v.tensor_scalar(m.mean[:], m.mean[:], 0.5, None, ALU.mult).then_inc(step, 1)
    v.scalar_tensor_tensor(m.diff[:], m.diff[:], 0.25, m.diff[:], ALU.mult, ALU.mult).then_inc(step, 1)
    v.tensor_scalar(m.ve[:], m.ve[:], 1.0 / H, EPS, ALU.mult, ALU.add).then_inc(step, 1)
    dve.wait_ge(step, base + ST + 6)
    v.tensor_tensor(m.ve[:], m.ve[:], m.diff[:], ALU.add).then_inc(ve_done, 1)
    dve.wait_ge(root_done, call + 1)
    v.reciprocal(m.inv[:], m.root[:]).then_inc(step, 1)
    dve.wait_ge(step, base + ST + 7)
    v.tensor_tensor(m.tmp[:], m.inv[:], m.inv[:], ALU.mult).then_inc(step, 1)
    dve.wait_ge(step, base + ST + 8)
    v.tensor_tensor(m.tmp[:], m.tmp[:], m.ve[:], ALU.mult).then_inc(step, 1)
    dve.wait_ge(step, base + ST + 9)
    v.tensor_scalar(m.tmp[:], m.tmp[:], -0.5, 1.5, ALU.mult, ALU.add).then_inc(step, 1)
    dve.wait_ge(step, base + ST + 10)
    v.tensor_tensor(m.inv[:], m.inv[:], m.tmp[:], ALU.mult).then_inc(step, 1)
    dve.wait_ge(step, base + ST + 11)


class Moments:

    def __init__(self, m):
        self.stats = m.sb("stats", [P, ST, 6])
        self.mean, self.diff, self.ve, self.root, self.inv, self.tmp = (
            m.sb(n, [P, ST]) for n in ("mean", "diff", "ve", "root", "inv", "tmp"))


def bcast(vec, n):
    return vec.rearrange("(o n) -> o n", o=1).to_broadcast([P, n])


def queries(nc, io, scr, wk, wv):
    with ExitStack() as stack:
        m = Mem(nc, stack, "q")
        ident = m.sb("ident", [P, P])
        had = m.sb("had", [P, P])
        wraw = m.sb("wraw", [P, 3, HC, H])
        wq = m.sb("wq", [P, 2, HC, H], F32R)
        bq = m.sb("bq", [P, HC])
        xt = m.sb("xt", [P, ST, H])
        xn = m.sb("xn", [P, ST, H])
        mo = Moments(m)
        xT = m.sb("xT", [P, 2, HC, S], F32R)
        qf = m.sb("qf", [P, HC, S])
        qs = m.sb("qs", [P, 2, HC, S], F32R)
        IC = INTER // P
        wd = [m.sb(f"wd{i}", [P, IC, H]) for i in range(2)]
        su_dp = m.sb("su_dp", [P, IC])
        wsc = m.sb("wsc", [P, H])
        wdf = m.sb("wdf", [P, 2, H])
        wds = m.sb("wds", [P, 2, 2, H], F32R)
        tp = [m.ps(f"tp{j}", [P, HC, P]) for j in range(2)]
        qp = [m.ps(f"qp{j}", [P, S]) for j in range(4)]
        dp = [m.ps(f"dp{j}", [P, H]) for j in range(2)]

        consts_in, weights_in, x_in, wd_in = m.sem("consts_in"), m.sem("weights_in"), m.sem("x_in"), m.sem("wd_in")
        split_hi, split_lo = m.sem("split_hi"), m.sem("split_lo")
        norm_step, ve_done, root_done = (m.sem(n) for n in ("norm_step", "ve_done", "root_done"))
        xn_done, tp_done, xh_done, xl_done = (m.sem(n) for n in ("xn_done", "tp_done", "xh_done", "xl_done"))
        q_done, qf_done, qh_done, ql_done, q_stored = (m.sem(n) for n in ("q_done", "qf_done", "qh_done", "ql_done", "q_stored"))
        fly, rot_done, wdf_done, wdh_done, wdl_done = (m.sem(n) for n in ("fly", "rot_done", "wdf_done", "wdh_done", "wdl_done"))
        wd_stored = m.sems("wd_stored", 2)
        wsc_done = m.sem("wsc_done")
        CONSTS = 5
        STAGES = IC.bit_length() - 1

        with nc.Block() as block:
            @block.sync
            def _(sp):
                sp.dma_start(wd[0][:], io["wdT"].rearrange("(c p) n -> p c n", p=P)).then_inc(wd_in, 16)
                sp.dma_start(ident[:], io["ident"]).then_inc(consts_in, 16)
                sp.dma_start(had[:], io["had"]).then_inc(consts_in, 16)
                sp.dma_start(bq[:], io["bq"]).then_inc(consts_in, 16)
                sp.dma_start(su_dp[:], io["su_dp"]).then_inc(consts_in, 16)
                sp.dma_start(wsc[:], bcast(io["ws_dp"], H)).then_inc(consts_in, 16)
                for i, w in enumerate(("wqT", "wkT", "wvT")):
                    sp.dma_start(wraw[:, i], io[w].rearrange("(c p) n -> p c n", p=P)).then_inc(weights_in, 16)
                with sp.Fori(0, B) as b:
                    sp.wait_ge(qh_done, b * HC)
                    sp.wait_ge(ql_done, b * HC)
                    sp.wait_ge(xn_done, b * ST)
                    sp.dma_start(xt[:], io["x"][b].rearrange("(n p) h -> p n h", p=P)).then_inc(x_in, 16)

            @block.gpsimd
            def _(pool):
                pool.wait_ge(wd_in, 16)
                for s in range(STAGES):
                    src, dst = wd[s % 2], wd[(s + 1) % 2]
                    a, z = 1 << (STAGES - 1 - s), 1 << s
                    si = src[:].rearrange("p (a two z) n -> p a two (z n)", two=2, z=z)
                    di = dst[:].rearrange("p (a two z) n -> p a two (z n)", two=2, z=z)
                    if s:
                        pool.wait_ge(fly, 2 * s)
                    nc.gpsimd.tensor_tensor(di[:, :, 0], si[:, :, 0], si[:, :, 1], ALU.add).then_inc(fly, 1)
                    nc.gpsimd.tensor_tensor(di[:, :, 1], si[:, :, 0], si[:, :, 1], ALU.subtract).then_inc(fly, 1)
                for c in range(IC):
                    pool.wait_ge(wdh_done, c + 1)
                    pool.wait_ge(wdl_done, c + 1)
                    pool.dma_start(scr["wd"][:, c], wds[:, c % 2].bitcast(F32)).then_inc(wd_stored[c % 2], 16)
                for i in range(2):
                    pool.wait_ge(wd_stored[i], 8 * IC)

            @block.scalar
            def _(act):
                act.wait_ge(weights_in, 48)
                for i, w in enumerate((wq, wk, wv)):
                    nc.scalar.activation(w[:, 0], wraw[:, i], ACT.Copy).then_inc(split_hi, 1)
                with act.Fori(0, B) as b:
                    act.wait_ge(ve_done, b + 1)
                    nc.scalar.activation(mo.root[:], mo.ve[:], ACT.Sqrt).then_inc(root_done, 1)
                    for j in range(ST):
                        act.wait_ge(tp_done, b * ST + j + 1)
                        if j == 0:
                            act.wait_ge(q_done, b * HC)
                        nc.scalar.activation(xT[:, 0, :, j * P:(j + 1) * P], tp[j % 2][:], ACT.Copy).then_inc(xh_done, 1)
                    for k in range(HC):
                        act.wait_ge(qf_done, b * HC + k + 1)
                        if k == 0:
                            act.wait_ge(q_stored, b * 32)
                        nc.scalar.activation(qs[:, 0, k], qf[:, k], ACT.Copy).then_inc(qh_done, 1)
                    act.wait_ge(qh_done, b * HC + HC)
                    act.dma_start(scr["q"][b, 0].rearrange("(c p) s -> p c s", p=P), qs[:, 0].bitcast(F32)).then_inc(q_stored, 16)
                    act.wait_ge(ql_done, b * HC + HC)
                    act.dma_start(scr["q"][b, 1].rearrange("(c p) s -> p c s", p=P), qs[:, 1].bitcast(F32)).then_inc(q_stored, 16)
                for c in range(IC):
                    act.wait_ge(wdf_done, c + 1)
                    if c >= 2:
                        act.wait_ge(wd_stored[c % 2], 16 * (c // 2))
                    nc.scalar.activation(wds[:, c % 2, 0], wdf[:, c % 2], ACT.Copy).then_inc(wdh_done, 1)
                act.wait_ge(q_stored, B * 32)

            @block.vector
            def _(dve):
                for i, w in enumerate((wq, wk, wv)):
                    dve.wait_ge(split_hi, i + 1)
                    nc.vector.tensor_tensor(w[:, 1], wraw[:, i], w[:, 0].bitcast(F32), ALU.subtract).then_inc(split_lo, 1)
                dve.wait_ge(consts_in, 16 * CONSTS)
                nc.vector.tensor_scalar(wsc[:], wsc[:], 1.0 / float(np.sqrt(INTER)), None, ALU.mult).then_inc(wsc_done, 1)
                with dve.Fori(0, B) as b:
                    row_moments(nc, dve, xt, lambda j: dve.wait_ge(x_in, b * 16 + 16) if j == 0 else None, norm_step,
                                b * NORM_STEPS, ve_done, root_done, b, mo)
                    for j in range(ST):
                        nc.vector.tensor_scalar(xn[:, j], xt[:, j], mo.mean[:, j:j + 1], mo.inv[:, j:j + 1],
                                                ALU.subtract, ALU.mult).then_inc(xn_done, 1)
                    for j in range(ST):
                        dve.wait_ge(xh_done, b * ST + j + 1)
                        cols = slice(j * P, (j + 1) * P)
                        nc.vector.tensor_tensor(xT[:, 1, :, cols], tp[j % 2][:], xT[:, 0, :, cols].bitcast(F32),
                                                ALU.subtract).then_inc(xl_done, 1)
                    for k in range(HC):
                        dve.wait_ge(q_done, b * HC + k + 1)
                        nc.vector.tensor_scalar(qf[:, k], qp[k][:], bq[:, k:k + 1], None, ALU.add).then_inc(qf_done, 1)
                    for k in range(HC):
                        dve.wait_ge(qh_done, b * HC + k + 1)
                        nc.vector.tensor_tensor(qs[:, 1, k], qf[:, k], qs[:, 0, k].bitcast(F32),
                                                ALU.subtract).then_inc(ql_done, 1)
                dve.wait_ge(wsc_done, 1)
                for c in range(IC):
                    dve.wait_ge(rot_done, c + 1)
                    if c >= 2:
                        dve.wait_ge(wdh_done, c - 1)
                    nc.vector.scalar_tensor_tensor(wdf[:, c % 2], dp[c % 2][:], su_dp[:, c:c + 1], wsc[:],
                                                   ALU.mult, ALU.mult).then_inc(wdf_done, 1)
                    dve.wait_ge(wdh_done, c + 1)
                    nc.vector.tensor_tensor(wds[:, c % 2, 1], wdf[:, c % 2], wds[:, c % 2, 0].bitcast(F32),
                                            ALU.subtract).then_inc(wdl_done, 1)

            @block.tensor
            def _(pe):
                pe.wait_ge(consts_in, 16 * CONSTS)
                pe.wait_ge(split_lo, 3)
                with pe.Fori(0, B) as b:
                    for j in range(ST):
                        pe.wait_ge(xn_done, b * ST + j + 1)
                        if j >= 2:
                            pe.wait_ge(xl_done, b * ST + j - 1)
                        for c in range(HC):
                            last = nc.tensor.transpose(tp[j % 2][:, c], xn[:, j, c * P:(c + 1) * P], ident[:])
                        last.then_inc(tp_done, 1)
                    pe.wait_ge(xl_done, b * ST + ST)
                    for k in range(HC):
                        pe.wait_ge(qf_done, b * HC)
                        last = split_product(nc, qp[k][:], lambda t, c: wq[:, t, c, k * P:(k + 1) * P],
                                             lambda t, c: xT[:, t, c, :])
                        last.then_inc(q_done, 1)
                pe.wait_ge(fly, 2 * STAGES)
                for c in range(IC):
                    if c >= 2:
                        pe.wait_ge(wdf_done, c - 1)
                    nc.tensor.matmul(dp[c % 2][:], had[:], wd[STAGES % 2][:, c], start=True, stop=True).then_inc(rot_done, 1)


def split_product(nc, out, stationary, moving, chunks=HC, first=True, final=True):
    parts = [(c, a, z) for c in range(chunks) for a, z in ((0, 0), (0, 1), (1, 0))]
    for n, (c, a, z) in enumerate(parts):
        last = nc.tensor.matmul(out, stationary(a, c), moving(z, c),
                                start=first and n == 0, stop=final and n == len(parts) - 1)
    return last


def keys_values(nc, io, scr, wk, wv):
    TILES = [3, 3, 3, TT - 9]
    FROM = [0, 3, 6, 9]
    WIDTH = [3 * P, 3 * P, 3 * P, TE - 9 * P]
    WMAX = max(WIDTH)
    NP = len(TILES)
    with ExitStack() as stack:
        m = Mem(nc, stack, "kv")
        bk = m.sb("bk", [P, HC])
        raw = [m.sb(f"raw{i}", [P, HC, WMAX]) for i in range(2)]
        cs = [m.sb(f"cs{i}", [P, 2, HC, WMAX], F32R) for i in range(2)]
        kf = m.sb("kf", [P, HC, WMAX])
        ks = m.sb("ks", [P, 2, HC, WMAX], F32R)
        vs = m.sb("vs", [P, NH, 4, 2 * HD])
        ones = m.sb("ones", [P, NH, HD])
        maski = m.sb("maski", [P, TE], I32)
        maskf = m.sb("maskf", [P, TE])
        mcoli = m.sb("mcoli", [P, TT], I32)
        mcol = m.sb("mcol", [P, TT])
        kp = [m.ps(f"kp{i}", [P, WMAX]) for i in range(4)]
        vp = [m.ps(f"vp{i}", [P, NH, HD]) for i in range(4)]

        consts_in, ready = m.sem("consts_in"), m.sem("ready")
        raw_in = m.sems("raw_in", 2)
        mask_in, mask_done, weight_step, weight_done = (m.sem(n) for n in ("mask_in", "mask_done", "weight_step", "weight_done"))
        hi_done, lo_done = m.sem("hi_done"), m.sem("lo_done")
        k_done, kf_done, kh_done, kl_done, k_stored = (m.sem(n) for n in ("k_done", "kf_done", "kh_done", "kl_done", "k_stored"))
        v_done, vs_done, vw_done, v_stored = (m.sem(n) for n in ("v_done", "vs_done", "vw_done", "v_stored"))
        V_DMAS = 5

        with nc.Block() as block:
            @block.sync
            def _(sp):
                sp.dma_start(bk[:], io["bk"]).then_inc(consts_in, 16)
                sp.wait_ge(ready, 4)
                with sp.Fori(0, B) as b:
                    sp.wait_ge(mask_done, b)
                    sp.wait_ge(weight_step, b)
                    row = io["mask"][b].rearrange("(o t) -> o t", o=1)
                    sp.dma_start(maski[:, 0:T], row.to_broadcast([P, T])).then_inc(mask_in, 16)
                    sp.dma_start(mcoli[:, 0:TT - 1], io["mask"][b, 0:(TT - 1) * P].rearrange("(n p) -> p n", p=P),
                                 allow_slow_non_contiguous=True).then_inc(mask_in, 16)
                    sp.dma_start(mcoli[0:TLAST, TT - 1:TT], io["mask"][b, (TT - 1) * P:T].rearrange("(p o) -> p o", o=1),
                                 allow_slow_non_contiguous=True).then_inc(mask_in, 16)
                    for p in range(NP):
                        if p >= 2:
                            sp.wait_ge(lo_done, b * NP + p - 1)
                        else:
                            sp.wait_ge(lo_done, b * NP)
                        t0 = FROM[p] * P
                        w = min(T - t0, WIDTH[p])
                        sp.dma_start(raw[p % 2][:, :, 0:w],
                                     io["ctxT"][b, :, t0:t0 + w].rearrange("(c p) t -> p c t", p=P)).then_inc(raw_in[p % 2], 16)

            @block.gpsimd
            def _(pool):
                nc.gpsimd.memset(ones[:], 1.0).then_inc(ready, 1)
                nc.gpsimd.memset(maski[:, T - 1:TE], 0).then_inc(ready, 1)
                nc.gpsimd.memset(mcoli[:], 0).then_inc(ready, 1)
                nc.gpsimd.memset(raw[(NP - 1) % 2][:, :, WMAX - 1:WMAX], 0.0).then_inc(ready, 1)
                pool.wait_ge(ready, 4)
                with pool.Fori(0, B) as b:
                    pool.wait_ge(weight_done, b + 1)
                    for p in range(NP):
                        for n in range(TILES[p]):
                            t = FROM[p] + n
                            if n == 0:
                                pool.wait_ge(v_stored, b * V_DMAS * 16 + p * 16)
                            nc.gpsimd.tensor_tensor(vs[:, :, n, HD:2 * HD], ones[:],
                                                    mcol[:, t:t + 1].unsqueeze(2).to_broadcast([P, NH, HD]),
                                                    ALU.mult).then_inc(vw_done, 1)
                        pool.wait_ge(vw_done, b * TT + FROM[p] + TILES[p])
                        pool.wait_ge(vs_done, b * TT + FROM[p] + TILES[p])
                        full = min(TILES[p], TT - 1 - FROM[p])
                        dst = scr["v"][b].rearrange("h p t w -> p h t w")
                        pool.dma_start(dst[:, :, FROM[p]:FROM[p] + full], vs[:, :, 0:full]).then_inc(v_stored, 16)
                        if full < TILES[p]:
                            pool.dma_start(dst[0:TLAST, :, TT - 1], vs[0:TLAST, :, full]).then_inc(v_stored, 16)
                pool.wait_ge(v_stored, B * V_DMAS * 16)

            @block.scalar
            def _(act):
                with act.Fori(0, B) as b:
                    for p in range(NP):
                        w = WIDTH[p]
                        act.wait_ge(raw_in[p % 2], (b * NP // 2 + p // 2 + 1) * 16)
                        act.wait_ge(v_done, b * TT + (FROM[p - 1] if p >= 2 else 0))
                        nc.scalar.activation(cs[p % 2][:, 0, :, 0:w], raw[p % 2][:, :, 0:w], ACT.Copy).then_inc(hi_done, 1)
                        for k in range(HC):
                            act.wait_ge(kf_done, (b * NP + p) * HC + k + 1)
                            if k == 0:
                                act.wait_ge(k_stored, (b * NP + p) * 32)
                            nc.scalar.activation(ks[:, 0, k, 0:w], kf[:, k, 0:w], ACT.Copy).then_inc(kh_done, 1)
                        for n in range(TILES[p]):
                            t = FROM[p] + n
                            act.wait_ge(v_done, b * TT + t + 1)
                            if n == 0:
                                act.wait_ge(weight_done, b + 1)
                                act.wait_ge(v_stored, b * V_DMAS * 16 + p * 16)
                            rows = TLAST if t == TT - 1 else P
                            nc.scalar.activation(vs[0:rows, :, n, 0:HD], vp[t % 4][0:rows], ACT.Copy,
                                                 scale=mcol[0:rows, t:t + 1]).then_inc(vs_done, 1)
                        act.wait_ge(kh_done, (b * NP + p) * HC + HC)
                        act.wait_ge(kl_done, (b * NP + p) * HC + HC)
                        t0 = FROM[p] * P
                        for half in range(2):
                            act.dma_start(scr["k"][b, half, :, t0:t0 + w].rearrange("(c p) t -> p c t", p=P),
                                          ks[:, half, :, 0:w].bitcast(F32)).then_inc(k_stored, 16)
                act.wait_ge(k_stored, B * NP * 32)

            @block.vector
            def _(dve):
                dve.wait_ge(consts_in, 16)
                with dve.Fori(0, B) as b:
                    dve.wait_ge(mask_in, b * 48 + 48)
                    nc.vector.tensor_scalar(maskf[:], maski[:], 0.5, None, ALU.is_gt).then_inc(mask_done, 1)
                    dve.wait_ge(vw_done, b * TT)
                    dve.wait_ge(vs_done, b * TT)
                    nc.vector.tensor_scalar(mcol[:], mcoli[:], 0.5, None, ALU.is_gt).then_inc(weight_step, 1)
                    dve.wait_ge(weight_step, b + 1)
                    nc.vector.tensor_scalar(mcol[:], mcol[:], 1.0 - LOW, LOW, ALU.mult, ALU.add).then_inc(weight_done, 1)
                    dve.wait_ge(mask_done, b + 1)
                    for p in range(NP):
                        w = WIDTH[p]
                        dve.wait_ge(hi_done, b * NP + p + 1)
                        nc.vector.tensor_tensor(cs[p % 2][:, 1, :, 0:w], raw[p % 2][:, :, 0:w],
                                                cs[p % 2][:, 0, :, 0:w].bitcast(F32), ALU.subtract).then_inc(lo_done, 1)
                        for k in range(HC):
                            dve.wait_ge(k_done, (b * NP + p) * HC + k + 1)
                            nc.vector.scalar_tensor_tensor(kf[:, k, 0:w], kp[k][:, 0:w], bk[:, k:k + 1],
                                                           maskf[:, FROM[p] * P:FROM[p] * P + w],
                                                           ALU.add, ALU.mult).then_inc(kf_done, 1)
                        for k in range(HC):
                            dve.wait_ge(kh_done, (b * NP + p) * HC + k + 1)
                            nc.vector.tensor_tensor(ks[:, 1, k, 0:w], kf[:, k, 0:w], ks[:, 0, k, 0:w].bitcast(F32),
                                                    ALU.subtract).then_inc(kl_done, 1)

            @block.tensor
            def _(pe):
                with pe.Fori(0, B) as b:
                    for p in range(NP):
                        w = WIDTH[p]
                        c0 = cs[p % 2]
                        pe.wait_ge(lo_done, b * NP + p + 1)
                        pe.wait_ge(kf_done, (b * NP + p) * HC)
                        for k in range(HC):
                            last = split_product(nc, kp[k][:, 0:w], lambda t, c: wk[:, t, c, k * P:(k + 1) * P],
                                                 lambda t, c: c0[:, t, c, 0:w])
                            last.then_inc(k_done, 1)
                        for n in range(TILES[p]):
                            t = FROM[p] + n
                            rows = TLAST if t == TT - 1 else P
                            if n == 0:
                                pe.wait_ge(vs_done, b * TT + t)
                            last = split_product(nc, vp[t % 4][0:rows], lambda z, c: c0[:, z, c, n * P:n * P + rows],
                                                 lambda z, c: wv[:, z, c, :])
                            last.then_inc(v_done, 1)


def attention(nc, scr):
    GROUPS = [3, 3, 3, 2, 2]
    FROM = [0, 3, 6, 9, 11]
    NG = len(GROUPS)
    PG = 2 * NG
    GMAX = max(GROUPS)
    NPROB = PG
    NSC = 2
    FULL = TT - 1
    K_DMAS, Q_DMAS, V_DMAS = 4, 4, 2
    SCALE = 1.0 / float(np.sqrt(HD))
    with ExitStack() as stack:
        m = Mem(nc, stack, "at")
        kst = [m.sb(f"kst{j}", [P, TP], F32R) for j in range(2)]
        qst = [m.sb(f"qst{j}", [P, S], F32R) for j in range(2)]
        vst = [m.sb(f"vst{j}", [P, TT, 2 * HD]) for j in range(2)]
        probs = [m.sb(f"probs{i}", [P, GMAX, S]) for i in range(NPROB)]
        rec = m.sb("rec", [HD, S])
        ob = [m.sb(f"ob{j}", [HD, S]) for j in range(2)]
        sc = [m.ps(f"sc{i}", [P, GMAX, S]) for i in range(NSC)]
        acc = [m.ps(f"acc{j}", [2 * HD, S]) for j in range(2)]

        pads = m.sem("pads")
        kq_in, v_in = m.sems("kq_in", 2), m.sems("v_in", 2)
        scores_done, values_done = m.sems("scores_done", 2), m.sems("values_done", 2)
        exp_done, clip_done, rec_done = m.sem("exp_done"), m.sem("clip_done"), m.sem("rec_done")
        acc_read, stored = m.sems("acc_read", 2), m.sems("stored", 2)

        with nc.Block() as block:
            @block.sync
            def _(sp):
                sp.wait_ge(pads, 2)
                with sp.Fori(0, B) as b:
                    with sp.Fori(0, NH // 2) as hp:
                        n = b * (NH // 2) + hp
                        for j in range(2):
                            h = hp * 2 + j
                            sp.wait_ge(scores_done[j], n * NG)
                            for rep in range(2):
                                for half in range(2):
                                    r = (rep * 2 + half) * HD
                                    sp.dma_start(kst[j][r:r + HD, 0:TE].bitcast(F32), scr["k4"][b, half, h]).then_inc(kq_in[j], 16)
                                    r = (half * 2 + rep) * HD
                                    sp.dma_start(qst[j][r:r + HD].bitcast(F32), scr["q4"][b, half, h]).then_inc(kq_in[j], 16)
                            sp.wait_ge(values_done[j], n * NG)
                            sp.dma_start(vst[j][:, 0:FULL], scr["v"][b, h, :, 0:FULL]).then_inc(v_in[j], 16)
                            sp.dma_start(vst[j][0:TLAST, FULL], scr["v"][b, h, 0:TLAST, FULL]).then_inc(v_in[j], 16)

            @block.gpsimd
            def _(pool):
                for j in range(2):
                    nc.gpsimd.memset(kst[j][:, TE:TP].bitcast(F32), 0.0).then_inc(pads, 1)
                with pool.Fori(0, B) as b:
                    with pool.Fori(0, NH // 2) as hp:
                        n = b * (NH // 2) + hp
                        for j in range(2):
                            pool.wait_ge(acc_read[j], n + 1)
                            pool.dma_start(scr["c4"][b, hp * 2 + j], ob[j][:]).then_inc(stored[j], 16)
                for j in range(2):
                    pool.wait_ge(stored[j], 16 * PAIRS)

            @block.scalar
            def _(act):
                with act.Fori(0, PAIRS) as n:
                    for g in range(PG):
                        size = GROUPS[g % NG]
                        act.wait_ge(scores_done[g // NG], n * NG + g % NG + 1)
                        act.wait_ge(values_done[g // NG], n * NG)
                        nc.scalar.activation(probs[g % NPROB][:, 0:size], sc[g % NSC][:, 0:size], ACT.Exp,
                                             scale=SCALE).then_inc(exp_done, 1)

            @block.vector
            def _(dve):
                def finish(n, j):
                    dve.wait_ge(values_done[j], (n + 1) * NG)
                    dve.wait_ge(stored[j], n * 16)
                    dve.wait_ge(acc_read[1 - j], n + j)
                    nc.vector.reciprocal(rec[:], acc[j][HD:2 * HD]).then_inc(rec_done, 1)
                    dve.wait_ge(rec_done, 2 * n + j + 1)
                    nc.vector.tensor_tensor(ob[j][:], acc[j][0:HD], rec[:], ALU.mult).then_inc(acc_read[j], 1)

                def pair(n, first):
                    for g in range(PG):
                        size = GROUPS[g % NG]
                        dve.wait_ge(exp_done, n * PG + g + 1)
                        p = probs[g % NPROB][:, 0:size]
                        nc.vector.tensor_scalar(p, p, LOW, HIGH, ALU.max, ALU.min).then_inc(clip_done, 1)
                        if g == 1 and not first:
                            finish(n - 1, 1)
                        if g == NG + 1:
                            finish(n, 0)

                pair(0, True)
                with dve.Fori(1, PAIRS) as n:
                    pair(n, False)
                finish(PAIRS - 1, 1)

            @block.tensor
            def _(pe):
                def scores(n, g, wait_slot=True):
                    j, k = g // NG, g % NG
                    if k == 0:
                        pe.wait_ge(kq_in[j], (n + 1) * 16 * (K_DMAS + Q_DMAS))
                    if wait_slot:
                        pe.wait_ge(exp_done, n * PG + g - NSC + 1)
                    for i in range(GROUPS[k]):
                        t = FROM[k] + i
                        last = nc.tensor.matmul(sc[g % NSC][:, i], kst[j][:, t * P:(t + 1) * P], qst[j][:],
                                                start=True, stop=True)
                    last.then_inc(scores_done[j], 1)

                def values(n, g):
                    j, k = g // NG, g % NG
                    if k == 0:
                        pe.wait_ge(v_in[j], (n + 1) * 16 * V_DMAS)
                        pe.wait_ge(acc_read[j], n)
                    pe.wait_ge(clip_done, n * PG + g + 1)
                    for i in range(GROUPS[k]):
                        t = FROM[k] + i
                        rows = TLAST if t == FULL else P
                        last = nc.tensor.matmul(acc[j][:], vst[j][0:rows, t], probs[g % NPROB][0:rows, i],
                                                start=t == 0, stop=t == FULL)
                    last.then_inc(values_done[j], 1)

                def pair(n, final):
                    for g in range(PG):
                        if g + 1 < PG:
                            scores(n, g + 1)
                        elif not final:
                            scores(n + 1, 0)
                        values(n, g)

                scores(0, 0, wait_slot=False)
                with pe.Fori(0, PAIRS - 1) as n:
                    pair(n, False)
                pair(PAIRS - 1, True)


def project(nc, io, scr):
    with ExitStack() as stack:
        m = Mem(nc, stack, "pr")
        ident, had = m.sb("ident", [P, P]), m.sb("had", [P, P])
        wraw = m.sb("wraw", [P, HC, H])
        wo = m.sb("wo", [P, 2, HC, H], F32R)
        bv, su = m.sb("bv", [P, HC]), m.sb("su", [P, HC])
        rs = m.sb("rs", [P, 1])
        bo, gamma, beta = m.sb("bo", [P, H]), m.sb("gamma", [P, H]), m.sb("beta", [P, H])
        craw, xt, xb = (m.sb(n, [P, ST, H]) for n in ("craw", "xt", "xb"))
        cf = m.sb("cf", [P, HC, S])
        cs = m.sb("cs", [P, 2, HC, S], F32R)
        d, x1 = m.sb("d", [P, ST, H]), m.sb("x1", [P, ST, H])
        mo = Moments(m)
        xT, xR = m.sb("xT", [P, HC, S]), m.sb("xR", [P, HC, S])
        xs = m.sb("xs", [P, 2, HC, S], F32R)
        op = [m.ps(f"op{j}", [P, H]) for j in range(4)]
        tp = [m.ps(f"tp{j}", [P, S]) for j in range(4)]

        (consts_in, w_in, c_in, x_in, w_hi, w_lo, rs_step, cf_done, c_hi, c_lo, o_done, d_done, xb_done, norm_step,
         ve_done, root_done, n_done, g_done, x1_done, x1_stored, xn_done, t_done, xT_done, fly, rot_done,
         xs_hi, xs_lo, xs_stored) = (m.sem(n) for n in (
             "consts_in", "w_in", "c_in", "x_in", "w_hi", "w_lo", "rs_step", "cf_done", "c_hi", "c_lo", "o_done",
             "d_done", "xb_done", "norm_step", "ve_done", "root_done", "n_done", "g_done", "x1_done",
             "x1_stored", "xn_done", "t_done", "xT_done", "fly", "rot_done", "xs_hi", "xs_lo", "xs_stored"))
        CONSTS = 8

        with nc.Block() as block:
            @block.sync
            def _(sp):
                sp.dma_start(wraw[:], io["woT"].rearrange("(c p) n -> p c n", p=P)).then_inc(w_in, 16)
                for t, src in ((ident, io["ident"]), (had, io["had"]), (bv, io["bv"]),
                               (su, io["su_ug"]), (rs, bcast(io["rs"], 1)),
                               (bo, bcast(io["bo"], H)), (gamma, bcast(io["gamma"], H)), (beta, bcast(io["beta"], H))):
                    sp.dma_start(t[:], src).then_inc(consts_in, 16)
                with sp.Fori(0, B) as b:
                    sp.wait_ge(cf_done, b * HC)
                    sp.dma_start(craw[:], scr["c"][b].rearrange("(c p) s -> p c s", p=P)).then_inc(c_in, 16)
                    sp.wait_ge(xb_done, b)
                    sp.dma_start(xt[:], io["x"][b].rearrange("(n p) h -> p n h", p=P)).then_inc(x_in, 16)

            @block.gpsimd
            def _(pool):
                pool.wait_ge(consts_in, 16 * CONSTS)
                with pool.Fori(0, B) as b:
                    pool.wait_ge(x_in, b * 16 + 16)
                    pool.wait_ge(x1_done, b * ST)
                    nc.gpsimd.tensor_tensor(xb[:], xt[:], beta[:].unsqueeze(1).to_broadcast([P, ST, H]), ALU.add).then_inc(xb_done, 1)
                    pool.wait_ge(x1_done, b * ST + ST)
                    pool.dma_start(scr["x1"][b], x1[:]).then_inc(x1_stored, 16)
                    for half, sem in enumerate((xs_hi, xs_lo)):
                        pool.wait_ge(sem, b * HC + HC)
                        pool.dma_start(scr["xs"][b, half], xs[:, half].bitcast(F32)).then_inc(xs_stored, 16)
                pool.wait_ge(x1_stored, B * 16)
                pool.wait_ge(xs_stored, B * 32)

            @block.scalar
            def _(act):
                act.wait_ge(w_in, 16)
                nc.scalar.activation(wo[:, 0], wraw[:], ACT.Copy).then_inc(w_hi, 1)
                with act.Fori(0, B) as b:
                    for c in range(HC):
                        act.wait_ge(cf_done, b * HC + c + 1)
                        if c == 0:
                            act.wait_ge(o_done, b * ST)
                        nc.scalar.activation(cs[:, 0, c], cf[:, c], ACT.Copy).then_inc(c_hi, 1)
                    for r in range(2):
                        act.wait_ge(ve_done, 2 * b + r + 1)
                        nc.scalar.activation(mo.root[:], mo.ve[:], ACT.Sqrt).then_inc(root_done, 1)
                    for c in range(HC):
                        act.wait_ge(rot_done, b * HC + c + 1)
                        if c == 0:
                            act.wait_ge(xs_stored, b * 32)
                        nc.scalar.activation(xs[:, 0, c], tp[c][:], ACT.Copy).then_inc(xs_hi, 1)

            @block.vector
            def _(dve):
                dve.wait_ge(w_hi, 1)
                nc.vector.tensor_tensor(wo[:, 1], wraw[:], wo[:, 0].bitcast(F32), ALU.subtract).then_inc(w_lo, 1)
                dve.wait_ge(consts_in, 16 * CONSTS)
                nc.vector.tensor_scalar(rs[:], rs[:], 0.0, 0.3, ALU.max, ALU.min).then_inc(rs_step, 1)
                dve.wait_ge(rs_step, 1)
                nc.vector.tensor_scalar(bo[:], bo[:], rs[:, 0:1], None, ALU.mult).then_inc(rs_step, 1)
                dve.wait_ge(rs_step, 2)
                with dve.Fori(0, B) as b:
                    dve.wait_ge(c_in, b * 16 + 16)
                    for c in range(HC):
                        nc.vector.tensor_scalar(cf[:, c], craw[:, c], bv[:, c:c + 1], None, ALU.add).then_inc(cf_done, 1)
                    for c in range(HC):
                        dve.wait_ge(c_hi, b * HC + c + 1)
                        nc.vector.tensor_tensor(cs[:, 1, c], cf[:, c], cs[:, 0, c].bitcast(F32), ALU.subtract).then_inc(c_lo, 1)
                    for j in range(ST):
                        dve.wait_ge(o_done, b * ST + j + 1)
                        nc.vector.scalar_tensor_tensor(d[:, j], op[j][:], rs[:, 0:1], bo[:], ALU.mult, ALU.add).then_inc(d_done, 1)

                    def norm(r, src, src_ready, dst, done):
                        row_moments(nc, dve, src, lambda j: dve.wait_ge(src_ready, b * ST + j + 1), norm_step,
                                    (2 * b + r) * NORM_STEPS, ve_done, root_done, 2 * b + r, mo)
                        for j in range(ST):
                            nc.vector.tensor_scalar(dst[:, j], src[:, j], mo.mean[:, j:j + 1], mo.inv[:, j:j + 1],
                                                    ALU.subtract, ALU.mult).then_inc(done, 1)

                    norm(0, d, d_done, d, n_done)
                    for j in range(ST):
                        dve.wait_ge(n_done, b * ST + j + 1)
                        nc.vector.tensor_tensor(d[:, j], d[:, j], gamma[:], ALU.mult).then_inc(g_done, 1)
                    dve.wait_ge(xb_done, b + 1)
                    dve.wait_ge(x1_stored, b * 16)
                    for j in range(ST):
                        dve.wait_ge(g_done, b * ST + j + 1)
                        nc.vector.tensor_tensor(x1[:, j], d[:, j], xb[:, j], ALU.add).then_inc(x1_done, 1)
                    norm(1, x1, x1_done, d, xn_done)
                    NORM = 1.0 / float(np.sqrt(H))
                    for c in range(HC):
                        dve.wait_ge(t_done, b * HC + c + 1)
                        nc.vector.tensor_scalar(xT[:, c], tp[c][:], su[:, c:c + 1], NORM, ALU.mult, ALU.mult).then_inc(xT_done, 1)
                    dve.wait_ge(xT_done, b * HC + HC)
                    for dst, src, ax in ((xR, xT, "p (two z) s -> p two z s"), (xT, xR, "p (z two) s -> p two z s")):
                        si, di = src[:].rearrange(ax, two=2), dst[:].rearrange(ax, two=2)
                        for k, alu in enumerate((ALU.add, ALU.subtract)):
                            nc.vector.tensor_tensor(di[:, k], si[:, 0], si[:, 1], alu).then_inc(fly, 1)
                        dve.wait_ge(fly, b * 4 + (2 if dst is xR else 4))
                    for c in range(HC):
                        dve.wait_ge(xs_hi, b * HC + c + 1)
                        nc.vector.tensor_tensor(xs[:, 1, c], tp[c][:], xs[:, 0, c].bitcast(F32), ALU.subtract).then_inc(xs_lo, 1)

            @block.tensor
            def _(pe):
                pe.wait_ge(w_lo, 1)
                pe.wait_ge(consts_in, 16 * CONSTS)
                with pe.Fori(0, B) as b:
                    pe.wait_ge(c_lo, b * HC + HC)
                    pe.wait_ge(d_done, b * ST)
                    for j in range(ST):
                        split_product(nc, op[j][:], lambda t, c: cs[:, t, c, j * P:(j + 1) * P],
                                      lambda t, c: wo[:, t, c, :]).then_inc(o_done, 1)
                    pe.wait_ge(xn_done, b * ST + ST)
                    pe.wait_ge(xs_lo, b * HC)
                    for c in range(HC):
                        for j in range(ST):
                            last = nc.tensor.transpose(tp[c][:, j * P:(j + 1) * P], d[:, j, c * P:(c + 1) * P], ident[:])
                        last.then_inc(t_done, 1)
                    pe.wait_ge(fly, b * 4 + 4)
                    for c in range(HC):
                        nc.tensor.matmul(tp[c][:], had[:], xT[:, c], start=True, stop=True).then_inc(rot_done, 1)


def at_least(eng, sem, value):
    if not (isinstance(value, int) and value <= 0):
        eng.wait_ge(sem, value)


def ffn(nc, io, scr, out):
    IC = 2
    GR = INTER // (IC * P)
    UN = B * IC
    with ExitStack() as stack:
        m = Mem(nc, stack, "ff")
        xs = m.sb("xs", [P, 2, B, HC, S], F32R)
        x1 = m.sb("x1", [P, B, ST, H])
        ugr = m.sb("ugr", [P, 2, HC, IC * P])
        ugs = [m.sb(f"ugs{i}", [P, 2, 2, HC, IC * P], F32R) for i in range(2)]
        wds = [m.sb(f"wds{i}", [P, IC, 2, H], F32R) for i in range(2)]
        scale = [m.sb(f"scale{i}", [P, 2, IC]) for i in range(2)]
        silu = [m.sb(f"silu{i}", [P, S]) for i in range(2)]
        hf = [m.sb(f"hf{i}", [P, S]) for i in range(2)]
        hs = [m.sb(f"hs{i}", [P, 2, S], F32R) for i in range(2)]
        up = [m.ps(f"up{i}", [P, S]) for i in range(2)]
        gp = [m.ps(f"gp{i}", [P, S]) for i in range(2)]
        yp = [m.ps(f"yp{i}", [P, H]) for i in range(ST)]

        (x1_in, ug_in, ug_hi, ug_lo, gate_done, silu_done, hf_done, h_hi, h_lo, down_done,
         y_read, out_stored) = (m.sem(n) for n in (
             "x1_in", "ug_in", "ug_hi", "ug_lo", "gate_done", "silu_done", "hf_done", "h_hi",
             "h_lo", "down_done", "y_read", "out_stored"))
        xs_in = m.sems("xs_in", B)
        wd_in = m.sems("wd_in", 2)
        assert GR % 2 == 0 and GR >= 6

        def in_pairs(eng, group):
            for k in range(2):
                group(k, k, False)
            with eng.Fori(1, GR // 2 - 1) as i:
                for k in range(2):
                    group(i * 2 + k, k, False)
            for k in range(2):
                group(GR - 2 + k, k, k == 1)

        with nc.Block() as block:
            @block.sync
            def _(sp):
                def load(g, k):
                    at_least(sp, ug_lo, g * 2)
                    for i, w in enumerate(("upT", "gateT")):
                        src = io[w].rearrange("(c p) n -> p c n", p=P)
                        sp.dma_start(ugr[:, i], src[:, :, bass.ds(g * IC * P, IC * P)]).then_inc(ug_in, 16)
                    at_least(sp, down_done, (g - 1) * UN)
                    sp.dma_start(wds[k][:].bitcast(F32), scr["wd"][:, bass.ds(g * IC, IC)]).then_inc(wd_in[k], 16)
                    sp.dma_start(scale[k][:], io["ws_ug"][:, :, bass.ds(g * IC, IC)]).then_inc(wd_in[k], 16)

                load(0, 0)
                for b in range(B):
                    sp.dma_start(xs[:, :, b].bitcast(F32), scr["xs"][b].rearrange("t p c s -> p t c s")).then_inc(xs_in[b], 16)
                sp.dma_start(x1[:], scr["x1"].rearrange("b p n h -> p b n h")).then_inc(x1_in, 16)
                load(1, 1)
                with sp.Fori(1, GR // 2) as i:
                    for k in range(2):
                        load(i * 2 + k, k)
                for b in range(B):
                    sp.wait_ge(y_read, ((GR - 1) * B + b + 1) * ST)
                    sp.dma_start(out[b].rearrange("(n p) h -> p n h", p=P), x1[:, b]).then_inc(out_stored, 16)
                sp.wait_ge(out_stored, B * 16)

            @block.scalar
            def _(act):
                def split_weights(g, k):
                    act.wait_ge(ug_in, (g + 1) * 32)
                    at_least(act, gate_done, (g - 1) * UN)
                    for i in range(2):
                        nc.scalar.activation(ugs[k][:, i, 0], ugr[:, i], ACT.Copy).then_inc(ug_hi, 1)

                def group(g, k, final):
                    act.wait_ge(wd_in[k], (g - k) * 16 + 32)
                    for u in range(UN):
                        n = g * UN + u
                        if u == 2 and not final:
                            split_weights(g + 1, 1 - k)
                        act.wait_ge(gate_done, n + 1)
                        at_least(act, hf_done, n - 1)
                        nc.scalar.activation(silu[u % 2][:], gp[u % 2][:], ACT.Silu,
                                             scale=scale[k][:, 1, u % IC:u % IC + 1]).then_inc(silu_done, 1)
                        act.wait_ge(hf_done, n + 1)
                        at_least(act, down_done, n - 1)
                        nc.scalar.activation(hs[u % 2][:, 0], hf[u % 2][:], ACT.Copy).then_inc(h_hi, 1)

                split_weights(0, 0)
                in_pairs(act, group)

            @block.vector
            def _(dve):
                def split_weights(g, k):
                    dve.wait_ge(ug_hi, (g + 1) * 2)
                    for i in range(2):
                        nc.vector.tensor_tensor(ugs[k][:, i, 1], ugr[:, i], ugs[k][:, i, 0].bitcast(F32),
                                                ALU.subtract).then_inc(ug_lo, 1)

                def accumulate(g, b):
                    dve.wait_ge(down_done, (g * B + b + 1) * IC)
                    if isinstance(g, int) and g == 0:
                        if b == 0:
                            dve.wait_ge(x1_in, 16)
                    else:
                        dve.wait_ge(y_read, ((g - 1) * B + b + 1) * ST)
                    for j in range(ST):
                        nc.vector.tensor_tensor(x1[:, b, j], yp[j][:], x1[:, b, j], ALU.add).then_inc(y_read, 1)

                def group(g, k, final):
                    dve.wait_ge(wd_in[k], (g - k) * 16 + 32)
                    for u in range(UN):
                        n = g * UN + u
                        if u == 2 and not final:
                            split_weights(g + 1, 1 - k)
                        dve.wait_ge(silu_done, n + 1)
                        at_least(dve, h_hi, n - 1)
                        nc.vector.scalar_tensor_tensor(hf[u % 2][:], up[u % 2][:], scale[k][:, 0, u % IC:u % IC + 1],
                                                       silu[u % 2][:], ALU.mult, ALU.mult).then_inc(hf_done, 1)
                        dve.wait_ge(h_hi, n + 1)
                        nc.vector.tensor_tensor(hs[u % 2][:, 1], hf[u % 2][:], hs[u % 2][:, 0].bitcast(F32),
                                                ALU.subtract).then_inc(h_lo, 1)
                        if u % IC == 0:
                            if u:
                                accumulate(g, u // IC - 1)
                            elif not (isinstance(g, int) and g == 0):
                                accumulate(g - 1, B - 1)

                split_weights(0, 0)
                in_pairs(dve, group)
                accumulate(GR - 1, B - 1)

            @block.tensor
            def _(pe):
                def gate_up(g, k, u):
                    b, i = u // IC, u % IC
                    if isinstance(g, int) and g == 0 and i == 0:
                        pe.wait_ge(xs_in[b], 16)
                    if u == 0:
                        pe.wait_ge(ug_lo, (g + 1) * 2)
                    at_least(pe, hf_done, g * UN + u - 1)
                    for w, acc in ((0, up), (1, gp)):
                        last = split_product(nc, acc[u % 2][:], lambda t, c: ugs[k][:, w, t, c, i * P:(i + 1) * P],
                                             lambda t, c: xs[:, t, b, c])
                    last.then_inc(gate_done, 1)

                def down(g, k, u):
                    b, i = u // IC, u % IC
                    if u == 0:
                        pe.wait_ge(wd_in[k], (g - k) * 16 + 32)
                    if i == 0:
                        at_least(pe, y_read, (g * B + b) * ST)
                    pe.wait_ge(h_lo, g * UN + u + 1)
                    for j in range(ST):
                        last = split_product(nc, yp[j][:], lambda t, c: hs[u % 2][:, t, j * P:(j + 1) * P],
                                             lambda t, c: wds[k][:, i, t], chunks=1, first=i == 0, final=i == IC - 1)
                    last.then_inc(down_done, 1)

                def group(g, k, final):
                    for u in range(UN):
                        if u + 1 < UN:
                            gate_up(g, k, u + 1)
                        elif not final:
                            gate_up(g + 1, 1 - k, 0)
                        down(g, k, u)

                gate_up(0, 0, 0)
                in_pairs(pe, group)


def build(nc, io, out):
    def scratch(name, shape, dt=F32):
        return nc.dram_tensor(f"scr_{name}", shape, dt).ap()

    scr = {
        "q": scratch("q", [B, 2, H, S]),
        "k": scratch("k", [B, 2, H, TE]),
        "v": scratch("v", [B, NH, P, TT, 2 * HD]),
        "c": scratch("c", [B, H, S]),
        "x1": scratch("x1", [B, P, ST, H]),
        "xs": scratch("xs", [B, 2, P, HC, S]),
        "wd": scratch("wd", [P, INTER // P, 2, H]),
    }
    scr["q4"] = scr["q"].rearrange("b t (h d) s -> b t h d s", d=HD)
    scr["k4"] = scr["k"].rearrange("b t (h d) s -> b t h d s", d=HD)
    scr["c4"] = scr["c"].rearrange("b (h d) s -> b h d s", d=HD)
    with ExitStack() as stack:
        m = Mem(nc, stack, "w")
        wk, wv = m.sb("wk", [P, 2, HC, H], F32R), m.sb("wv", [P, 2, HC, H], F32R)
        queries(nc, io, scr, wk, wv)
        keys_values(nc, io, scr, wk, wv)
    attention(nc, scr)
    project(nc, io, scr)
    ffn(nc, io, scr, out)


def hadamard(n):
    h = np.ones((1, 1), np.float32)
    while h.shape[0] < n:
        h = np.block([[h, h], [h, -h]])
    return np.ascontiguousarray(h.astype(np.float32))


def kernel(**inputs):
    import concourse.bacc as bacc
    from concourse.bass_utils import run_bass_kernel_spmd

    a = {k: np.asarray(v) for k, v in inputs.items()}
    def columns(v):
        return v.reshape(-1, P).T

    arrays = {
        "x": a["x"],
        "ctxT": a["ctx_2048"].transpose(0, 2, 1),
        "mask": a["mask_BxS2_ik0"],
        "bq": columns(a["L0_xattn_bq"]), "bk": columns(a["L0_xattn_bk"]), "bv": columns(a["L0_xattn_bv"]),
        "bo": a["L0_xattn_bo"],
        "wqT": a["L0_xattn_Wq"].T, "wkT": a["L0_xattn_Wk"].T, "wvT": a["L0_xattn_Wv"].T, "woT": a["L0_xattn_Wo"].T,
        "gamma": a["L0_xattn_ln_gamma"], "beta": a["L0_xattn_ln_beta"],
        "rs": a["L0_xattn_residual_scale"].reshape(1),
        "su_ug": columns(a["L0_ffn_SU_ug"]), "su_dp": columns(a["L0_ffn_SU_dp"]),
        "ws_ug": columns(a["L0_ffn_Wscale_ug"]).reshape(P, 2, INTER // P), "ws_dp": a["L0_ffn_Wscale_dp"],
        "upT": a["L0_ffn_W_up"].T, "gateT": a["L0_ffn_W_gate"].T, "wdT": a["L0_ffn_W_down"].T,
        "ident": np.eye(P, dtype=np.float32), "had": hadamard(P),
    }
    arrays = {f"in_{k}": np.ascontiguousarray(v) for k, v in arrays.items()}
    nc = bacc.Bacc("TRN2", target_bir_lowering=False, num_devices=1)
    io = {k[3:]: nc.dram_tensor(k, v.shape, mybir.dt.from_np(v.dtype), kind="ExternalInput").ap()
          for k, v in arrays.items()}
    out = nc.dram_tensor("out", (B, S, H), F32, kind="ExternalOutput").ap()
    build(nc, io, out)
    r = run_bass_kernel_spmd(nc, [arrays], core_ids=[0])
    return r.results[0]["out"]
```

```python
import numpy as np
import concourse.bass as bass
from concourse import mybir
from contextlib import ExitStack

F32 = mybir.dt.float32
F32R = mybir.dt.float32r
I32 = mybir.dt.int32
ALU = mybir.AluOpType
ACT = mybir.ActivationFunctionType

B, S, H, T = 4, 512, 512, 1601
NH = 16
HD = H // NH
INTER = 2048
P = 128
HC = H // P
ST = S // P
TT = -(-T // P)
TLAST = T - (TT - 1) * P
TE = T + T % 2
TP = TT * P
LOW = float(np.float32(np.exp(-50.0)))
HIGH = float(np.float32(np.exp(50.0)))
EPS = 1e-5
PAIRS = B * NH // 2


class Mem:

    def __init__(self, nc, stack, prefix):
        self.nc, self.stack, self.prefix = nc, stack, prefix

    def sb(self, name, shape, dt=F32):
        return self.stack.enter_context(self.nc.sbuf_tensor(f"{self.prefix}_{name}", shape, dt))

    def ps(self, name, shape, dt=F32):
        return self.stack.enter_context(self.nc.psum_tensor(f"{self.prefix}_{name}", shape, dt))

    def sem(self, name):
        return self.stack.enter_context(self.nc.semaphore(f"{self.prefix}_{name}"))

    def sems(self, name, n):
        return [self.sem(f"{name}{i}") for i in range(n)]


NORM_STEPS = ST + 11


def row_moments(nc, dve, src, src_wait, step, base, ve_done, root_done, call, m):
    v = nc.vector
    for j in range(ST):
        src_wait(j)
        v.bn_stats(m.stats[:, j], src[:, j]).then_inc(step, 1)
    st = m.stats[:].rearrange("p j (o k) -> p k o j", o=2)
    mean, m2 = st[:, 1], st[:, 2]
    dve.wait_ge(step, base + ST)
    v.tensor_tensor(m.mean[:], mean[:, 0], mean[:, 1], ALU.add).then_inc(step, 1)
    v.tensor_tensor(m.diff[:], mean[:, 0], mean[:, 1], ALU.subtract).then_inc(step, 1)
    v.tensor_tensor(m.ve[:], m2[:, 0], m2[:, 1], ALU.add).then_inc(step, 1)
    dve.wait_ge(step, base + ST + 3)
    v.tensor_scalar(m.mean[:], m.mean[:], 0.5, None, ALU.mult).then_inc(step, 1)
    v.scalar_tensor_tensor(m.diff[:], m.diff[:], 0.25, m.diff[:], ALU.mult, ALU.mult).then_inc(step, 1)
    v.tensor_scalar(m.ve[:], m.ve[:], 1.0 / H, EPS, ALU.mult, ALU.add).then_inc(step, 1)
    dve.wait_ge(step, base + ST + 6)
    v.tensor_tensor(m.ve[:], m.ve[:], m.diff[:], ALU.add).then_inc(ve_done, 1)
    dve.wait_ge(root_done, call + 1)
    v.reciprocal(m.inv[:], m.root[:]).then_inc(step, 1)
    dve.wait_ge(step, base + ST + 7)
    v.tensor_tensor(m.tmp[:], m.inv[:], m.inv[:], ALU.mult).then_inc(step, 1)
    dve.wait_ge(step, base + ST + 8)
    v.tensor_tensor(m.tmp[:], m.tmp[:], m.ve[:], ALU.mult).then_inc(step, 1)
    dve.wait_ge(step, base + ST + 9)
    v.tensor_scalar(m.tmp[:], m.tmp[:], -0.5, 1.5, ALU.mult, ALU.add).then_inc(step, 1)
    dve.wait_ge(step, base + ST + 10)
    v.tensor_tensor(m.inv[:], m.inv[:], m.tmp[:], ALU.mult).then_inc(step, 1)
    dve.wait_ge(step, base + ST + 11)


class Moments:

    def __init__(self, m):
        self.stats = m.sb("stats", [P, ST, 6])
        self.mean, self.diff, self.ve, self.root, self.inv, self.tmp = (
            m.sb(n, [P, ST]) for n in ("mean", "diff", "ve", "root", "inv", "tmp"))


def bcast(vec, n):
    return vec.rearrange("(o n) -> o n", o=1).to_broadcast([P, n])


def at_least(eng, sem, value):
    if not (isinstance(value, int) and value <= 0):
        eng.wait_ge(sem, value)


def split_product(nc, out, stationary, moving, chunks=HC, first=True, final=True):
    parts = [(c, a, z) for c in range(chunks) for a, z in ((0, 0), (0, 1), (1, 0))]
    for n, (c, a, z) in enumerate(parts):
        last = nc.tensor.matmul(out, stationary(a, c), moving(z, c),
                                start=first and n == 0, stop=final and n == len(parts) - 1)
    return last


def prepare(nc, io, scr):
    TILES = [3, 3, 3, TT - 9]
    FROM = [0, 3, 6, 9]
    WIDTH = [3 * P, 3 * P, 3 * P, TE - 9 * P]
    WMAX = max(WIDTH)
    NP = len(TILES)
    NORM, TRANS, QUERY = 1, 2, 3
    VD = 2 * HD + 2
    with ExitStack() as stack:
        m = Mem(nc, stack, "pp")
        ident = m.sb("ident", [P, P])
        wraw = [m.sb(f"wraw{i}", [P, HC, H]) for i in range(2)]
        wk, wv, wq = (m.sb(n, [P, 2, HC, H], F32R) for n in ("wk", "wv", "wq"))
        bk, bq = m.sb("bk", [P, HC]), m.sb("bq", [P, HC])
        raw = [m.sb(f"raw{i}", [P, HC, WMAX]) for i in range(2)]
        cs = [m.sb(f"cs{i}", [P, 2, HC, WMAX], F32R) for i in range(2)]
        kf = m.sb("kf", [P, HC, WMAX])
        ks = m.sb("ks", [P, 2, HC, WMAX], F32R)
        vf = [m.sb(f"vf{i}", [P, NH, HD]) for i in range(2)]
        vs = m.sb("vs", [P, NH, 4, VD], F32R)
        maski, maskf = m.sb("maski", [P, TE], I32), m.sb("maskf", [P, TE])
        mcoli, mcol = m.sb("mcoli", [P, TT], I32), m.sb("mcol", [P, TT])
        wcol = m.sb("wcol", [P, TT, 2], F32R)
        ones = m.sb("ones", [P, NH, 4, 2])
        xt = m.sb("xt", [P, ST, H])
        mo = Moments(m)
        xT = m.sb("xT", [P, 2, HC, S], F32R)
        qf = [m.sb(f"qf{i}", [P, S]) for i in range(2)]
        qs = [m.sb(f"qs{i}", [P, 2, S], F32R) for i in range(2)]
        kp = [m.ps(f"kp{i}", [P, WMAX]) for i in range(2)]
        vp = [m.ps(f"vp{i}", [P, NH, HD]) for i in range(2)]
        tp = [m.ps(f"tp{i}", [P, HC, P]) for i in range(2)]
        qp = [m.ps(f"qp{i}", [P, S]) for i in range(2)]

        consts_in, pads = m.sem("consts_in"), m.sem("pads")
        w_in, w_hi, w_lo = m.sems("w_in", 3), m.sem("w_hi"), m.sem("w_lo")
        raw_in = m.sems("raw_in", 2)
        mask_in, mask_done, weight_step, weight_done, wcol_done, wcopy_done = (m.sem(n) for n in (
            "mask_in", "mask_done", "weight_step", "weight_done", "wcol_done", "wcopy_done"))
        c_hi, c_lo = m.sem("c_hi"), m.sem("c_lo")
        k_done, kf_done, k_hi, k_lo, k_stored = (m.sem(n) for n in ("k_done", "kf_done", "k_hi", "k_lo", "k_stored"))
        v_done, vf_done, v_hi, v_lo, v_stored = (m.sem(n) for n in ("v_done", "vf_done", "v_hi", "v_lo", "v_stored"))
        x_in, norm_step, ve_done, root_done, xn_done, t_done, x_hi, x_lo = (m.sem(n) for n in (
            "x_in", "norm_step", "ve_done", "root_done", "xn_done", "t_done", "x_hi", "x_lo"))
        q_done, qf_done, q_hi, q_lo = (m.sem(n) for n in ("q_done", "qf_done", "q_hi", "q_lo"))
        q_stored = m.sems("q_stored", 2)
        V_DMAS = 5

        def over_batches(eng, batch):
            with eng.Fori(0, B - 1) as b:
                batch(b, False)
            batch(B - 1, True)

        with nc.Block() as block:
            @block.sync
            def _(sp):
                def weights(i, w):
                    sp.dma_start(wraw[i % 2][:], io[w].rearrange("(c p) n -> p c n", p=P)).then_inc(w_in[i], 16)

                def context(b, p):
                    t0 = FROM[p] * P
                    w = min(T - t0, WIDTH[p])
                    sp.dma_start(raw[p % 2][:, :, 0:w],
                                 io["ctxT"][b, :, t0:t0 + w].rearrange("(c p) t -> p c t", p=P)).then_inc(raw_in[p % 2], 16)

                weights(0, "wkT")
                for t, src in ((bk, "bk"), (bq, "bq"), (ident, "ident")):
                    sp.dma_start(t[:], io[src]).then_inc(consts_in, 16)
                weights(1, "wvT")
                sp.wait_ge(pads, 4)
                with sp.Fori(0, B) as b:
                    for p in range(NP):
                        sp.wait_ge(c_lo, b * NP + max(p - 1, 0))
                        context(b, p)
                        if p == 0:
                            sp.wait_ge(mask_done, b)
                            sp.wait_ge(weight_step, b)
                            row = io["mask"][b].rearrange("(o t) -> o t", o=1)
                            sp.dma_start(maski[:, 0:T], row.to_broadcast([P, T])).then_inc(mask_in, 16)
                            sp.dma_start(mcoli[:, 0:TT - 1], io["mask"][b, 0:(TT - 1) * P].rearrange("(n p) -> p n", p=P),
                                         allow_slow_non_contiguous=True).then_inc(mask_in, 16)
                            sp.dma_start(mcoli[0:TLAST, TT - 1:TT], io["mask"][b, (TT - 1) * P:T].rearrange("(p o) -> p o", o=1),
                                         allow_slow_non_contiguous=True).then_inc(mask_in, 16)
                        if p == 1:
                            sp.wait_ge(t_done, b * ST)
                            sp.dma_start(xt[:], io["x"][b].rearrange("(n p) h -> p n h", p=P)).then_inc(x_in, 16)

            @block.gpsimd
            def _(pool):
                nc.gpsimd.memset(maski[:, T - 1:TE], 0).then_inc(pads, 1)
                nc.gpsimd.memset(mcoli[:], 0).then_inc(pads, 1)
                nc.gpsimd.memset(ones[:], 1.0).then_inc(pads, 1)
                nc.gpsimd.memset(raw[(NP - 1) % 2][:, :, WMAX - 1:WMAX], 0.0).then_inc(pads, 1)
                pool.wait_ge(w_lo, 1)
                pool.dma_start(wraw[0][:], io["wqT"].rearrange("(c p) n -> p c n", p=P)).then_inc(w_in[2], 16)
                with pool.Fori(0, B) as b:
                    for p in range(NP):
                        n, t = TILES[p], FROM[p]
                        if p == 0:
                            pool.wait_ge(wcol_done, 2 * b + 2)
                            pool.wait_ge(pads, 4)
                        pool.wait_ge(v_stored, (b * V_DMAS + p) * 16)
                        both = wcol[:, t:t + n].bitcast(F32).unsqueeze(1).to_broadcast([P, NH, n, 2])
                        nc.gpsimd.tensor_tensor(vs[:, :, 0:n, 2 * HD:VD], both, ones[:, :, 0:n], ALU.mult).then_inc(wcopy_done, 1)
                        pool.wait_ge(wcopy_done, b * NP + p + 1)
                        pool.wait_ge(v_lo, b * TT + t + n)
                        full = min(n, TT - 1 - t)
                        dst = scr["v"][b].rearrange("h p t w -> p h t w")
                        pool.dma_start(dst[:, :, t:t + full], vs[:, :, 0:full].bitcast(F32)).then_inc(v_stored, 16)
                        if full < n:
                            pool.dma_start(dst[0:TLAST, :, TT - 1], vs[0:TLAST, :, full].bitcast(F32)).then_inc(v_stored, 16)
                pool.wait_ge(v_stored, B * V_DMAS * 16)

            @block.scalar
            def _(act):
                def weights(i, w):
                    act.wait_ge(w_in[i], 16)
                    nc.scalar.activation(w[:, 0], wraw[i % 2][:], ACT.Copy).then_inc(w_hi, 1)

                def context(b, p):
                    w = WIDTH[p]
                    act.wait_ge(raw_in[p % 2], b * (NP // 2 * 16) + (p // 2 + 1) * 16)
                    nc.scalar.activation(cs[p % 2][:, 0, :, 0:w], raw[p % 2][:, :, 0:w], ACT.Copy).then_inc(c_hi, 1)

                def batch(b, final):
                    for p in range(NP):
                        w = WIDTH[p]
                        if p + 1 < NP:
                            context(b, p + 1)
                        elif not final:
                            context(b + 1, 0)
                        if p == NORM:
                            act.wait_ge(ve_done, b + 1)
                            nc.scalar.activation(mo.root[:], mo.ve[:], ACT.Sqrt).then_inc(root_done, 1)
                        for k in range(HC):
                            act.wait_ge(kf_done, (b * NP + p) * HC + k + 1)
                            if k == 0:
                                act.wait_ge(k_stored, (b * NP + p) * 32)
                            nc.scalar.activation(ks[:, 0, k, 0:w], kf[:, k, 0:w], ACT.Copy).then_inc(k_hi, 1)
                            if p == TRANS:
                                act.wait_ge(t_done, b * ST + k + 1)
                                if k == 0:
                                    act.wait_ge(q_done, b * HC)
                                nc.scalar.activation(xT[:, 0, :, k * P:(k + 1) * P], tp[k % 2][:], ACT.Copy).then_inc(x_hi, 1)
                            if p == QUERY:
                                act.wait_ge(qf_done, b * HC + k + 1)
                                act.wait_ge(q_stored[k % 2], (b * 2 + k // 2) * 32)
                                nc.scalar.activation(qs[k % 2][:, 0], qf[k % 2][:], ACT.Copy).then_inc(q_hi, 1)
                                act.wait_ge(q_hi, b * HC + k + 1)
                                act.wait_ge(q_lo, b * HC + k + 1)
                                for half in range(2):
                                    act.dma_start(scr["q"][half, b, k * P:(k + 1) * P], qs[k % 2][:, half].bitcast(F32)
                                                  ).then_inc(q_stored[k % 2], 16)
                        if p == 0:
                            act.wait_ge(weight_done, b + 1)
                        for n in range(TILES[p]):
                            t = FROM[p] + n
                            i = b * TT + t
                            act.wait_ge(v_done, i + 1)
                            act.wait_ge(v_lo, i - 1 if t else i)
                            rows = TLAST if t == TT - 1 else P
                            nc.scalar.activation(vf[t % 2][0:rows], vp[t % 2][0:rows], ACT.Copy,
                                                 scale=mcol[0:rows, t:t + 1]).then_inc(vf_done, 1)
                            if n == 0:
                                act.wait_ge(v_stored, (b * V_DMAS + p) * 16)
                            act.wait_ge(vf_done, i + 1)
                            nc.scalar.activation(vs[0:rows, :, n, 0:HD], vf[t % 2][0:rows], ACT.Copy).then_inc(v_hi, 1)
                        act.wait_ge(k_hi, (b * NP + p) * HC + HC)
                        act.wait_ge(k_lo, (b * NP + p) * HC + HC)
                        t0 = FROM[p] * P
                        for half in range(2):
                            act.dma_start(scr["k"][half, b, :, t0:t0 + w].rearrange("(c p) t -> p c t", p=P),
                                          ks[:, half, :, 0:w].bitcast(F32)).then_inc(k_stored, 16)

                weights(0, wk)
                context(0, 0)
                weights(1, wv)
                weights(2, wq)
                over_batches(act, batch)
                act.wait_ge(k_stored, B * NP * 32)
                for i in range(2):
                    act.wait_ge(q_stored[i], B * 64)

            @block.vector
            def _(dve):
                def weights(i, w):
                    dve.wait_ge(w_hi, i + 1)
                    nc.vector.tensor_tensor(w[:, 1], wraw[i % 2][:], w[:, 0].bitcast(F32), ALU.subtract).then_inc(w_lo, 1)

                def context(b, p):
                    w = WIDTH[p]
                    dve.wait_ge(c_hi, b * NP + p + 1)
                    nc.vector.tensor_tensor(cs[p % 2][:, 1, :, 0:w], raw[p % 2][:, :, 0:w],
                                            cs[p % 2][:, 0, :, 0:w].bitcast(F32), ALU.subtract).then_inc(c_lo, 1)

                def masks(b):
                    dve.wait_ge(mask_in, b * 48 + 48)
                    nc.vector.tensor_scalar(maskf[:], maski[:], 0.5, None, ALU.is_gt).then_inc(mask_done, 1)
                    dve.wait_ge(vf_done, b * TT)
                    dve.wait_ge(wcopy_done, b * NP)
                    nc.vector.tensor_scalar(mcol[:], mcoli[:], 0.5, None, ALU.is_gt).then_inc(weight_step, 1)
                    dve.wait_ge(weight_step, b + 1)
                    nc.vector.tensor_scalar(mcol[:], mcol[:], 1.0 - LOW, LOW, ALU.mult, ALU.add).then_inc(weight_done, 1)
                    dve.wait_ge(weight_done, b + 1)
                    nc.vector.tensor_copy(wcol[:, :, 0], mcol[:]).then_inc(wcol_done, 1)
                    dve.wait_ge(wcol_done, 2 * b + 1)
                    nc.vector.tensor_tensor(wcol[:, :, 1], mcol[:], wcol[:, :, 0].bitcast(F32), ALU.subtract).then_inc(wcol_done, 1)
                    dve.wait_ge(mask_done, b + 1)

                def key_lo(b, p, k):
                    w = WIDTH[p]
                    dve.wait_ge(k_hi, (b * NP + p) * HC + k + 1)
                    nc.vector.tensor_tensor(ks[:, 1, k, 0:w], kf[:, k, 0:w], ks[:, 0, k, 0:w].bitcast(F32),
                                            ALU.subtract).then_inc(k_lo, 1)

                def batch(b, final):
                    masks(b)
                    for p in range(NP):
                        w = WIDTH[p]
                        if p + 1 < NP:
                            context(b, p + 1)
                        elif not final:
                            context(b + 1, 0)
                        if p == NORM:
                            row_moments(nc, dve, xt, lambda j: dve.wait_ge(x_in, b * 16 + 16) if j == 0 else None,
                                        norm_step, b * NORM_STEPS, ve_done, root_done, b, mo)
                            for j in range(ST):
                                nc.vector.tensor_scalar(xt[:, j], xt[:, j], mo.mean[:, j:j + 1], mo.inv[:, j:j + 1],
                                                        ALU.subtract, ALU.mult).then_inc(xn_done, 1)
                        for k in range(HC):
                            dve.wait_ge(k_done, (b * NP + p) * HC + k + 1)
                            nc.vector.scalar_tensor_tensor(kf[:, k, 0:w], kp[k % 2][:, 0:w], bk[:, k:k + 1],
                                                           maskf[:, FROM[p] * P:FROM[p] * P + w],
                                                           ALU.add, ALU.mult).then_inc(kf_done, 1)
                            if k:
                                key_lo(b, p, k - 1)
                            if p == TRANS:
                                dve.wait_ge(x_hi, b * ST + k + 1)
                                cols = slice(k * P, (k + 1) * P)
                                nc.vector.tensor_tensor(xT[:, 1, :, cols], tp[k % 2][:], xT[:, 0, :, cols].bitcast(F32),
                                                        ALU.subtract).then_inc(x_lo, 1)
                            if p == QUERY:
                                dve.wait_ge(q_done, b * HC + k + 1)
                                dve.wait_ge(q_lo, b * HC + k - 1 if k else b * HC)
                                nc.vector.tensor_scalar(qf[k % 2][:], qp[k % 2][:], bq[:, k:k + 1], None, ALU.add).then_inc(qf_done, 1)
                                dve.wait_ge(q_hi, b * HC + k + 1)
                                nc.vector.tensor_tensor(qs[k % 2][:, 1], qf[k % 2][:], qs[k % 2][:, 0].bitcast(F32),
                                                        ALU.subtract).then_inc(q_lo, 1)
                        key_lo(b, p, HC - 1)
                        for n in range(TILES[p]):
                            t = FROM[p] + n
                            rows = TLAST if t == TT - 1 else P
                            dve.wait_ge(v_hi, b * TT + t + 1)
                            nc.vector.tensor_tensor(vs[0:rows, :, n, HD:2 * HD], vf[t % 2][0:rows],
                                                    vs[0:rows, :, n, 0:HD].bitcast(F32), ALU.subtract).then_inc(v_lo, 1)

                weights(0, wk)
                context(0, 0)
                weights(1, wv)
                weights(2, wq)
                dve.wait_ge(consts_in, 16 * 3)
                over_batches(dve, batch)

            @block.tensor
            def _(pe):
                pe.wait_ge(w_lo, 1)
                pe.wait_ge(consts_in, 16 * 3)
                with pe.Fori(0, B) as b:
                    for p in range(NP):
                        w = WIDTH[p]
                        c0 = cs[p % 2]
                        pe.wait_ge(c_lo, b * NP + p + 1)
                        for k in range(HC):
                            i = p * HC + k
                            pe.wait_ge(kf_done, b * NP * HC + (i - 1 if i else 0))
                            split_product(nc, kp[k % 2][:, 0:w], lambda t, c: wk[:, t, c, k * P:(k + 1) * P],
                                          lambda t, c: c0[:, t, c, 0:w]).then_inc(k_done, 1)
                            if p == TRANS:
                                if k == 0:
                                    pe.wait_ge(xn_done, b * ST + ST)
                                pe.wait_ge(x_lo, b * ST + (k - 1 if k else 0))
                                for c in range(HC):
                                    last = nc.tensor.transpose(tp[k % 2][:, c], xt[:, k, c * P:(c + 1) * P], ident[:])
                                last.then_inc(t_done, 1)
                            if p == QUERY:
                                if k == 0:
                                    pe.wait_ge(w_lo, 3)
                                    pe.wait_ge(x_lo, b * ST + ST)
                                pe.wait_ge(qf_done, b * HC + (k - 1 if k else 0))
                                split_product(nc, qp[k % 2][:], lambda t, c: wq[:, t, c, k * P:(k + 1) * P],
                                              lambda t, c: xT[:, t, c, :]).then_inc(q_done, 1)
                        if p == 0:
                            pe.wait_ge(w_lo, 2)
                        for n in range(TILES[p]):
                            t = FROM[p] + n
                            rows = TLAST if t == TT - 1 else P
                            pe.wait_ge(vf_done, b * TT + (t - 1 if t else 0))
                            split_product(nc, vp[t % 2][0:rows], lambda z, c: c0[:, z, c, n * P:n * P + rows],
                                          lambda z, c: wv[:, z, c, :]).then_inc(v_done, 1)


def attention(nc, io, scr):
    GROUPS = [3, 2, 3, 3, 2]
    FROM = [0, 3, 5, 8, 11]
    SPLIT = [True, False, True, True, False]
    NG = len(GROUPS)
    PG = 2 * NG
    GMAX = max(GROUPS)
    NSC = 2
    AHEAD = NG + 1
    UNROLL = 3
    FULL = TT - 1
    SCALE = 1.0 / float(np.sqrt(HD))
    VD = 2 * HD + 2
    SLOT = {g: i for i, g in enumerate(g for g in range(PG) if SPLIT[g % NG])}
    with ExitStack() as stack:
        m = Mem(nc, stack, "at")
        kst = [m.sb(f"kst{j}", [P, TP], F32R) for j in range(2)]
        qst = [m.sb(f"qst{j}", [P, S], F32R) for j in range(2)]
        vst = [m.sb(f"vst{j}", [P, TT, VD], F32R) for j in range(2)]
        probs = [m.sb(f"probs{i}", [P, GROUPS[i % NG], S]) for i in range(PG)]
        parts = [m.sb(f"parts{i}", [P, 2, GMAX, S], F32R) for i in range(len(SLOT))]
        ob = [m.sb(f"ob{j}", [VD, S]) for j in range(2)]
        sc = [m.ps(f"sc{i}", [P, GMAX, S]) for i in range(NSC)]
        acc = [m.ps(f"acc{j}", [VD, S]) for j in range(2)]

        pads = m.sem("pads")
        kq_in, v_in = m.sems("kq_in", 2), m.sems("v_in", 2)
        scores_done, values_done = m.sems("scores_done", 2), m.sems("values_done", 2)
        exp_done, clip_done, p_hi, p_lo = (m.sem(n) for n in ("exp_done", "clip_done", "p_hi", "p_lo"))
        acc_read, stored = m.sems("acc_read", 2), m.sems("stored", 2)
        fly_in, fly, fly_out = (m.sem(n) for n in ("fly_in", "fly", "fly_out"))
        NS = len(SLOT)
        IC = INTER // P
        STAGES = IC.bit_length() - 1
        wd = [m.sb(f"wd{i}", [P, IC, H // 2]) for i in range(2)]

        with nc.Block() as block:
            @block.sync
            def _(sp):
                def keys(n, j):
                    h = n * 2 + j
                    at_least(sp, scores_done[j], n * NG)
                    for i in range(2):
                        rows = slice(i * 2 * HD, (i + 1) * 2 * HD)
                        sp.dma_start(kst[j][rows, 0:TE].bitcast(F32), scr["k4"][:, h]).then_inc(kq_in[j], 16)
                        sp.dma_start(qst[j][rows].bitcast(F32), scr["q4"][i, h].unsqueeze(0).to_broadcast([2, HD, S])
                                     ).then_inc(kq_in[j], 16)

                def weights(n, j):
                    h = n * 2 + j
                    at_least(sp, values_done[j], n * NG)
                    sp.dma_start(vst[j][:, 0:FULL].bitcast(F32), scr["v4"][h, :, 0:FULL]).then_inc(v_in[j], 16)
                    sp.dma_start(vst[j][0:TLAST, FULL].bitcast(F32), scr["v4"][h, 0:TLAST, FULL]).then_inc(v_in[j], 16)

                def store(n, j):
                    h = n * 2 + j
                    sp.wait_ge(acc_read[j], n + 1)
                    sp.dma_start(scr["c4"][0, h], ob[j][0:HD]).then_inc(stored[j], 16)
                    sp.dma_start(scr["c4"][1, h], ob[j][HD:2 * HD]).then_inc(stored[j], 16)
                    sp.dma_start(scr["sum4"][:, h], ob[j][2 * HD:VD]).then_inc(stored[j], 16)

                def turn(n, second):
                    keys(n, 0)
                    weights(n - 1, 1)
                    if not second:
                        store(n - 2, 1)
                    keys(n, 1)
                    weights(n, 0)
                    store(n - 1, 0)

                sp.wait_ge(pads, 2)
                keys(0, 0)
                weights(0, 0)
                keys(0, 1)
                turn(1, True)
                with sp.Fori(2, PAIRS) as n:
                    turn(n, False)
                weights(PAIRS - 1, 1)
                store(PAIRS - 2, 1)
                for j in range(2):
                    store(PAIRS - 1, j)
                for j in range(2):
                    sp.wait_ge(stored[j], 48 * PAIRS)

            @block.gpsimd
            def _(pool):
                for j in range(2):
                    nc.gpsimd.memset(kst[j][:, TE:TP].bitcast(F32), 0.0).then_inc(pads, 1)
                for half in range(2):
                    cols = slice(half * (H // 2), (half + 1) * (H // 2))
                    base = half * 2 * STAGES
                    if half:
                        pool.wait_ge(fly, base)
                        pool.wait_ge(fly_out, 16)
                    pool.dma_start(wd[0][:], io["wdT"].rearrange("(c p) n -> p c n", p=P)[:, :, cols]).then_inc(fly_in, 16)
                    pool.wait_ge(fly_in, 16 * (half + 1))
                    for s in range(STAGES):
                        src, dst = wd[s % 2], wd[(s + 1) % 2]
                        z = 1 << s
                        si = src[:].rearrange("p (a two z) n -> p a two (z n)", two=2, z=z)
                        di = dst[:].rearrange("p (a two z) n -> p a two (z n)", two=2, z=z)
                        if s:
                            pool.wait_ge(fly, base + 2 * s)
                        nc.gpsimd.tensor_tensor(di[:, :, 0], si[:, :, 0], si[:, :, 1], ALU.add).then_inc(fly, 1)
                        nc.gpsimd.tensor_tensor(di[:, :, 1], si[:, :, 0], si[:, :, 1], ALU.subtract).then_inc(fly, 1)
                    pool.wait_ge(fly, base + 2 * STAGES)
                    pool.dma_start(scr["wdb"][:, :, cols], wd[STAGES % 2][:]).then_inc(fly_out, 16)
                pool.wait_ge(fly_out, 32)

            @block.scalar
            def _(act):
                def exp(n, g):
                    act.wait_ge(scores_done[g // NG], n * NG + g % NG + 1)
                    if g in SLOT:
                        at_least(act, p_lo, (n - 1) * NS + SLOT[g] + 1)
                    else:
                        at_least(act, values_done[g // NG], n * NG)
                    nc.scalar.activation(probs[g][:], sc[g % NSC][:, 0:GROUPS[g % NG]], ACT.Exp, scale=SCALE).then_inc(exp_done, 1)

                def split_hi(n, g):
                    if g in SLOT:
                        act.wait_ge(clip_done, n * PG + g + 1)
                        at_least(act, values_done[g // NG], n * NG)
                        nc.scalar.activation(parts[SLOT[g]][:, 0], probs[g][:], ACT.Copy).then_inc(p_hi, 1)

                def pair(n, first):
                    for g in range(PG):
                        exp(n, g)
                        if g >= 2:
                            split_hi(n, g - 2)
                        elif not first:
                            split_hi(n - 1, g + PG - 2)

                pair(0, True)
                with act.Fori(0, (PAIRS - 1) // UNROLL) as i:
                    for r in range(UNROLL):
                        pair(i * UNROLL + (1 + r), False)
                for n in range(PAIRS - (PAIRS - 1) % UNROLL, PAIRS):
                    pair(n, False)
                for g in (PG - 2, PG - 1):
                    split_hi(PAIRS - 1, g)

            @block.vector
            def _(dve):
                def collect(n, j):
                    dve.wait_ge(values_done[j], (n + 1) * NG)
                    dve.wait_ge(stored[j], n * 48)
                    nc.vector.tensor_copy(ob[j][:], acc[j][:]).then_inc(acc_read[j], 1)

                def split_lo(n, g):
                    if g in SLOT:
                        part = parts[SLOT[g]]
                        dve.wait_ge(p_hi, n * NS + SLOT[g] + 1)
                        nc.vector.tensor_tensor(part[:, 1], probs[g][:], part[:, 0].bitcast(F32), ALU.subtract).then_inc(p_lo, 1)

                def pair(n, first):
                    for g in range(PG):
                        dve.wait_ge(exp_done, n * PG + g + 1)
                        nc.vector.tensor_scalar(probs[g][:], probs[g][:], LOW, HIGH, ALU.max, ALU.min).then_inc(clip_done, 1)
                        if g >= 2:
                            split_lo(n, g - 2)
                        elif not first:
                            split_lo(n - 1, g + PG - 2)
                        if g == 4 and not first:
                            collect(n - 1, 1)
                        if g == NG + 4:
                            collect(n, 0)

                pair(0, True)
                with dve.Fori(1, PAIRS) as n:
                    pair(n, False)
                for g in (PG - 2, PG - 1):
                    split_lo(PAIRS - 1, g)
                collect(PAIRS - 1, 1)

            @block.tensor
            def _(pe):
                def scores(n, g):
                    j, k = g // NG, g % NG
                    if k == 0:
                        pe.wait_ge(kq_in[j], (n + 1) * 64)
                    at_least(pe, exp_done, n * PG + g - NSC + 1)
                    for i in range(GROUPS[k]):
                        t = FROM[k] + i
                        last = nc.tensor.matmul(sc[g % NSC][:, i], kst[j][:, t * P:(t + 1) * P], qst[j][:],
                                                start=True, stop=True)
                    last.then_inc(scores_done[j], 1)

                def values(n, g):
                    j, k = g // NG, g % NG
                    if k == 0:
                        pe.wait_ge(v_in[j], (n + 1) * 32)
                        pe.wait_ge(acc_read[j], n)
                    if g in SLOT:
                        pe.wait_ge(p_lo, n * NS + SLOT[g] + 1)
                    else:
                        pe.wait_ge(clip_done, n * PG + g + 1)
                    for i in range(GROUPS[k]):
                        t = FROM[k] + i
                        rows = TLAST if t == FULL else P
                        weights = vst[j][0:rows, t]
                        if g in SLOT:
                            for z in range(2):
                                last = nc.tensor.matmul(acc[j][:], weights, parts[SLOT[g]][0:rows, z, i],
                                                        start=t == 0 and z == 0, stop=t == FULL and z == 1)
                        else:
                            last = nc.tensor.matmul(acc[j][:], weights.bitcast(F32), probs[g][0:rows, i],
                                                    start=t == 0, stop=t == FULL)
                    last.then_inc(values_done[j], 1)

                def pair(n, final):
                    for g in range(PG):
                        if g + AHEAD < PG:
                            scores(n, g + AHEAD)
                        elif not final:
                            scores(n + 1, g + AHEAD - PG)
                        values(n, g)

                for g in range(AHEAD):
                    scores(0, g)
                with pe.Fori(0, PAIRS - 1) as n:
                    pair(n, False)
                pair(PAIRS - 1, True)


def project(nc, io, scr):
    IC = INTER // P
    with ExitStack() as stack:
        m = Mem(nc, stack, "pr")
        ident, had = m.sb("ident", [P, P]), m.sb("had", [P, P])
        wraw = m.sb("wraw", [P, HC, H])
        wo = m.sb("wo", [P, 2, HC, H], F32R)
        bv, su, su_dp = m.sb("bv", [P, HC]), m.sb("su", [P, HC]), m.sb("su_dp", [P, IC])
        bvb = m.sb("bvb", [P, HC, P])
        rs = m.sb("rs", [P, 1])
        bo, gamma, beta, wsc = (m.sb(n, [P, H]) for n in ("bo", "gamma", "beta", "wsc"))
        SUMS = B * NH * S // P
        sums, recip = m.sb("sums", [P, 2, SUMS]), m.sb("recip", [P, SUMS])
        ca, cb, rb = (m.sb(n, [P, HC, S]) for n in ("ca", "cb", "rb"))
        cs = m.sb("cs", [P, 2, HC, S], F32R)
        xt, d, x1 = (m.sb(n, [P, ST, H]) for n in ("xt", "d", "x1"))
        mo = Moments(m)
        xT, xR = m.sb("xT", [P, HC, S]), m.sb("xR", [P, HC, S])
        xs = m.sb("xs", [P, 2, HC, S], F32R)
        wd = m.sb("wd", [P, IC, H])
        wdf = m.sb("wdf", [P, 2, H])
        wds = m.sb("wds", [P, 4, 2, H], F32R)
        op = [m.ps(f"op{j}", [P, H]) for j in range(4)]
        tp = [m.ps(f"tp{j}", [P, S]) for j in range(4)]

        (consts_in, w_in, wd_in, sum_in, rec_out, w_hi, w_lo, bvb_done, bias_done, rs_step, rec_step, ab_in, r_in, x_in,
         ab_done, c_done, c_hi, c_lo, o_done, d_done, beta_done, norm_step, ve_done, root_done, n_done, g_done, x1_done,
         x1_stored, xn_done, t_done, xT_done, fly, rot_done, xs_hi, xs_lo, xs_stored, wrot_done, wdf_done, wd_hi,
         wd_lo) = (m.sem(n) for n in (
             "consts_in", "w_in", "wd_in", "sum_in", "rec_out", "w_hi", "w_lo", "bvb_done", "bias_done", "rs_step",
             "rec_step", "ab_in", "r_in", "x_in", "ab_done", "c_done", "c_hi", "c_lo", "o_done", "d_done", "beta_done",
             "norm_step", "ve_done", "root_done", "n_done", "g_done", "x1_done", "x1_stored", "xn_done", "t_done",
             "xT_done", "fly", "rot_done", "xs_hi", "xs_lo", "xs_stored", "wrot_done", "wdf_done", "wd_hi", "wd_lo"))
        wd_stored = m.sems("wd_stored", 4)
        CONSTS = 10

        def over_batches(eng, batch):
            with eng.Fori(0, B - 1) as b:
                batch(b, False)
            batch(B - 1, True)

        with nc.Block() as block:
            @block.sync
            def _(sp):
                def heads(b):
                    sp.wait_ge(c_lo, b * HC)
                    for t, half in ((ca, 0), (cb, 1)):
                        sp.dma_start(t[:], scr["c"][half, b].rearrange("(c p) s -> p c s", p=P)).then_inc(ab_in, 16)
                    for c in range(HC):
                        src = scr["rec"][b, 4 * c:4 * c + 4].unsqueeze(1).to_broadcast([4, HD, S])
                        sp.dma_start(rb[:, c], src).then_inc(r_in, 16)

                def rows(b):
                    sp.wait_ge(x1_done, b * ST)
                    sp.dma_start(xt[:], io["x"][b].rearrange("(n p) h -> p n h", p=P)).then_inc(x_in, 16)

                sp.dma_start(sums[:], scr["sum"].rearrange("z (p f) -> p z f", p=P)).then_inc(sum_in, 16)
                sp.dma_start(wraw[:], io["woT"].rearrange("(c p) n -> p c n", p=P)).then_inc(w_in, 16)
                for t, src in ((ident, io["ident"]), (had, io["had"]), (bv, io["bv"]), (su, io["su_ug"]),
                               (su_dp, io["su_dp"]), (rs, bcast(io["rs"], 1)), (bo, bcast(io["bo"], H)),
                               (gamma, bcast(io["gamma"], H)), (beta, bcast(io["beta"], H)), (wsc, bcast(io["ws_dp"], H))):
                    sp.dma_start(t[:], src).then_inc(consts_in, 16)
                sp.wait_ge(rec_step, 2)
                sp.dma_start(scr["rec"].rearrange("b h s -> (b h s)").rearrange("(p f) -> p f", p=P), recip[:]).then_inc(rec_out, 16)
                sp.wait_ge(rec_out, 16)
                with sp.Fori(0, B) as b:
                    heads(b)
                    rows(b)
                sp.dma_start(wd[:], scr["wdb"]).then_inc(wd_in, 16)

            @block.gpsimd
            def _(pool):
                def join(b):
                    pool.wait_ge(ab_in, b * 32 + 32)
                    nc.gpsimd.tensor_tensor(ca[:], ca[:], cb[:], ALU.add).then_inc(ab_done, 1)

                def rows(b):
                    pool.wait_ge(x_in, b * 16 + 16)
                    nc.gpsimd.tensor_tensor(xt[:], xt[:], beta[:].unsqueeze(1).to_broadcast([P, ST, H]), ALU.add).then_inc(beta_done, 1)

                def batch(b, final):
                    if not final:
                        join(b + 1)
                    pool.wait_ge(x1_done, b * ST + ST)
                    pool.dma_start(scr["x1"][b], x1[:]).then_inc(x1_stored, 16)
                    if not final:
                        rows(b + 1)
                    for half, sem in enumerate((xs_hi, xs_lo)):
                        pool.wait_ge(sem, b * HC + HC)
                        pool.dma_start(scr["xs"][b, half], xs[:, half].bitcast(F32)).then_inc(xs_stored, 16)

                join(0)
                pool.wait_ge(consts_in, 16 * CONSTS)
                rows(0)
                over_batches(pool, batch)
                pool.wait_ge(x1_stored, B * 16)
                pool.wait_ge(xs_stored, B * 32)
                for c in range(IC):
                    pool.wait_ge(wd_lo, c + 1)
                    pool.dma_start(scr["wd"][:, c], wds[:, c % 4].bitcast(F32)).then_inc(wd_stored[c % 4], 16)
                for i in range(4):
                    pool.wait_ge(wd_stored[i], 4 * IC)

            @block.scalar
            def _(act):
                def front(b):
                    for c in range(HC):
                        act.wait_ge(c_done, b * HC + c + 1)
                        if c == 0:
                            act.wait_ge(o_done, b * ST)
                        nc.scalar.activation(cs[:, 0, c], ca[:, c], ACT.Copy).then_inc(c_hi, 1)

                def batch(b, final):
                    for r in range(2):
                        act.wait_ge(ve_done, 2 * b + r + 1)
                        nc.scalar.activation(mo.root[:], mo.ve[:], ACT.Sqrt).then_inc(root_done, 1)
                    if not final:
                        front(b + 1)
                    for c in range(HC):
                        act.wait_ge(t_done, b * HC + c + 1)
                        nc.scalar.activation(xT[:, c], tp[c][:], ACT.Copy, scale=su[:, c:c + 1]).then_inc(xT_done, 1)
                    for c in range(HC):
                        act.wait_ge(rot_done, b * HC + c + 1)
                        if c == 0:
                            act.wait_ge(xs_stored, b * 32)
                        nc.scalar.activation(xs[:, 0, c], tp[c][:], ACT.Copy).then_inc(xs_hi, 1)

                act.wait_ge(w_in, 16)
                nc.scalar.activation(wo[:, 0], wraw[:], ACT.Copy).then_inc(w_hi, 1)
                front(0)
                act.wait_ge(rs_step, 5)
                over_batches(act, batch)
                for c in range(IC):
                    act.wait_ge(wdf_done, c + 1)
                    if c >= 4:
                        act.wait_ge(wd_stored[c % 4], 16 * (c // 4))
                    nc.scalar.activation(wds[:, c % 4, 0], wdf[:, c % 2], ACT.Copy).then_inc(wd_hi, 1)

            @block.vector
            def _(dve):
                def front(b):
                    dve.wait_ge(r_in, (b + 1) * 16 * HC)
                    dve.wait_ge(ab_done, b + 1)
                    for c in range(HC):
                        nc.vector.tensor_tensor(ca[:, c], ca[:, c], rb[:, c], ALU.mult).then_inc(c_done, 1)
                    for c in range(HC):
                        dve.wait_ge(c_hi, b * HC + c + 1)
                        nc.vector.tensor_tensor(cs[:, 1, c], ca[:, c], cs[:, 0, c].bitcast(F32), ALU.subtract).then_inc(c_lo, 1)

                def norm(b, r, src, src_ready, dst, done):
                    row_moments(nc, dve, src, lambda j: dve.wait_ge(src_ready, b * ST + j + 1), norm_step,
                                (2 * b + r) * NORM_STEPS, ve_done, root_done, 2 * b + r, mo)
                    for j in range(ST):
                        nc.vector.tensor_scalar(dst[:, j], src[:, j], mo.mean[:, j:j + 1], mo.inv[:, j:j + 1],
                                                ALU.subtract, ALU.mult).then_inc(done, 1)

                def batch(b, final):
                    for j in range(ST):
                        dve.wait_ge(o_done, b * ST + j + 1)
                        nc.vector.scalar_tensor_tensor(d[:, j], op[j][:], rs[:, 0:1], bo[:], ALU.mult, ALU.add).then_inc(d_done, 1)
                    norm(b, 0, d, d_done, d, n_done)
                    for j in range(ST):
                        dve.wait_ge(n_done, b * ST + j + 1)
                        nc.vector.tensor_tensor(d[:, j], d[:, j], gamma[:], ALU.mult).then_inc(g_done, 1)
                    dve.wait_ge(beta_done, b + 1)
                    dve.wait_ge(x1_stored, b * 16)
                    for j in range(ST):
                        dve.wait_ge(g_done, b * ST + j + 1)
                        nc.vector.tensor_tensor(x1[:, j], d[:, j], xt[:, j], ALU.add).then_inc(x1_done, 1)
                    norm(b, 1, x1, x1_done, d, xn_done)
                    if not final:
                        front(b + 1)
                    dve.wait_ge(xT_done, b * HC + HC)
                    for dst, src, ax in ((xR, xT, "p (two z) s -> p two z s"), (xT, xR, "p (z two) s -> p two z s")):
                        si, di = src[:].rearrange(ax, two=2), dst[:].rearrange(ax, two=2)
                        for k, alu in enumerate((ALU.add, ALU.subtract)):
                            nc.vector.tensor_tensor(di[:, k], si[:, 0], si[:, 1], alu).then_inc(fly, 1)
                        dve.wait_ge(fly, b * 4 + (2 if dst is xR else 4))
                    for c in range(HC):
                        dve.wait_ge(xs_hi, b * HC + c + 1)
                        nc.vector.tensor_tensor(xs[:, 1, c], tp[c][:], xs[:, 0, c].bitcast(F32), ALU.subtract).then_inc(xs_lo, 1)

                def split_down(c):
                    dve.wait_ge(wd_hi, c + 1)
                    nc.vector.tensor_tensor(wds[:, c % 4, 1], wdf[:, c % 2], wds[:, c % 4, 0].bitcast(F32),
                                            ALU.subtract).then_inc(wd_lo, 1)

                dve.wait_ge(sum_in, 16)
                nc.vector.tensor_tensor(sums[:, 0], sums[:, 0], sums[:, 1], ALU.add).then_inc(rec_step, 1)
                dve.wait_ge(rec_step, 1)
                nc.vector.reciprocal(recip[:], sums[:, 0]).then_inc(rec_step, 1)
                dve.wait_ge(w_hi, 1)
                nc.vector.tensor_tensor(wo[:, 1], wraw[:], wo[:, 0].bitcast(F32), ALU.subtract).then_inc(w_lo, 1)
                dve.wait_ge(consts_in, 16 * CONSTS)
                nc.vector.tensor_copy(bvb[:], bv[:].unsqueeze(2).to_broadcast([P, HC, P])).then_inc(bvb_done, 1)
                nc.vector.tensor_scalar(rs[:], rs[:], 0.0, 0.3, ALU.max, ALU.min).then_inc(rs_step, 1)
                nc.vector.tensor_scalar(su[:], su[:], 1.0 / float(np.sqrt(H)), None, ALU.mult).then_inc(rs_step, 1)
                nc.vector.tensor_scalar(wsc[:], wsc[:], 1.0 / float(np.sqrt(INTER)), None, ALU.mult).then_inc(rs_step, 1)
                dve.wait_ge(bias_done, 1)
                nc.vector.tensor_tensor(bo[:], tp[0][:], bo[:], ALU.add).then_inc(rs_step, 1)
                dve.wait_ge(rs_step, 4)
                nc.vector.tensor_scalar(bo[:], bo[:], rs[:, 0:1], None, ALU.mult).then_inc(rs_step, 1)
                dve.wait_ge(rs_step, 5)
                front(0)
                over_batches(dve, batch)
                for c in range(IC):
                    dve.wait_ge(wrot_done, c + 1)
                    if c >= 2:
                        dve.wait_ge(wd_lo, c - 1)
                    nc.vector.scalar_tensor_tensor(wdf[:, c % 2], tp[c % 4][:], su_dp[:, c:c + 1], wsc[:],
                                                   ALU.mult, ALU.mult).then_inc(wdf_done, 1)
                    if c:
                        split_down(c - 1)
                split_down(IC - 1)

            @block.tensor
            def _(pe):
                def out_proj(b, tiles):
                    for j in tiles:
                        if j == 0:
                            pe.wait_ge(c_lo, b * HC + HC)
                            pe.wait_ge(d_done, b * ST)
                        split_product(nc, op[j][:], lambda t, c: cs[:, t, c, j * P:(j + 1) * P],
                                      lambda t, c: wo[:, t, c, :]).then_inc(o_done, 1)

                def batch(b, final):
                    pe.wait_ge(xn_done, b * ST + ST)
                    pe.wait_ge(xs_lo, b * HC)
                    for c in range(HC):
                        for j in range(ST):
                            last = nc.tensor.transpose(tp[c][:, j * P:(j + 1) * P], d[:, j, c * P:(c + 1) * P], ident[:])
                        last.then_inc(t_done, 1)
                    if not final:
                        out_proj(b + 1, (0, 1))
                    pe.wait_ge(fly, b * 4 + 4)
                    for c in range(HC):
                        nc.tensor.matmul(tp[c][:], had[:], xT[:, c], start=True, stop=True).then_inc(rot_done, 1)
                    if not final:
                        out_proj(b + 1, (2, 3))

                pe.wait_ge(bvb_done, 1)
                for c in range(HC):
                    last = nc.tensor.matmul(tp[0][:], bvb[:, c], wraw[:, c], start=c == 0, stop=c == HC - 1)
                last.then_inc(bias_done, 1)
                pe.wait_ge(rs_step, 4)
                pe.wait_ge(w_lo, 1)
                out_proj(0, range(ST))
                over_batches(pe, batch)
                pe.wait_ge(wd_in, 16)
                for c in range(IC):
                    if c < 4:
                        pe.wait_ge(xs_lo, B * HC)
                    else:
                        pe.wait_ge(wdf_done, c - 3)
                    nc.tensor.matmul(tp[c % 4][:], had[:], wd[:, c], start=True, stop=True).then_inc(wrot_done, 1)


def ffn(nc, io, scr, out):
    IC = 2
    GR = INTER // (IC * P)
    UN = B * IC
    with ExitStack() as stack:
        m = Mem(nc, stack, "ff")
        xs = m.sb("xs", [P, 2, B, HC, S], F32R)
        x1 = m.sb("x1", [P, B, ST, H])
        ugr = m.sb("ugr", [P, 2, HC, IC * P])
        ugs = [m.sb(f"ugs{i}", [P, 2, 2, HC, IC * P], F32R) for i in range(2)]
        wds = [m.sb(f"wds{i}", [P, IC, 2, H], F32R) for i in range(2)]
        scale = [m.sb(f"scale{i}", [P, 2, IC]) for i in range(2)]
        silu = [m.sb(f"silu{i}", [P, S]) for i in range(2)]
        hf = [m.sb(f"hf{i}", [P, S]) for i in range(2)]
        hs = [m.sb(f"hs{i}", [P, 2, S], F32R) for i in range(2)]
        up = [m.ps(f"up{i}", [P, S]) for i in range(2)]
        gp = [m.ps(f"gp{i}", [P, S]) for i in range(2)]
        yp = [m.ps(f"yp{i}", [P, H]) for i in range(ST)]

        (x1_in, ug_in, ug_hi, ug_lo, gate_done, silu_done, hf_done, h_hi, h_lo, down_done,
         y_read, out_stored) = (m.sem(n) for n in (
             "x1_in", "ug_in", "ug_hi", "ug_lo", "gate_done", "silu_done", "hf_done", "h_hi",
             "h_lo", "down_done", "y_read", "out_stored"))
        xs_in = m.sems("xs_in", B)
        wd_in = m.sems("wd_in", 2)
        assert GR % 2 == 0 and GR >= 6

        def in_pairs(eng, group):
            for k in range(2):
                group(k, k, False)
            with eng.Fori(1, GR // 2 - 1) as i:
                for k in range(2):
                    group(i * 2 + k, k, False)
            for k in range(2):
                group(GR - 2 + k, k, k == 1)

        with nc.Block() as block:
            @block.sync
            def _(sp):
                def load(g, k):
                    at_least(sp, ug_lo, g * 2)
                    for i, w in enumerate(("upT", "gateT")):
                        src = io[w].rearrange("(c p) n -> p c n", p=P)
                        sp.dma_start(ugr[:, i], src[:, :, bass.ds(g * IC * P, IC * P)]).then_inc(ug_in, 16)
                    at_least(sp, down_done, (g - 1) * UN)
                    sp.dma_start(wds[k][:].bitcast(F32), scr["wd"][:, bass.ds(g * IC, IC)]).then_inc(wd_in[k], 16)
                    sp.dma_start(scale[k][:], io["ws_ug"][:, :, bass.ds(g * IC, IC)]).then_inc(wd_in[k], 16)

                load(0, 0)
                for b in range(B):
                    sp.dma_start(xs[:, :, b].bitcast(F32), scr["xs"][b].rearrange("t p c s -> p t c s")).then_inc(xs_in[b], 16)
                sp.dma_start(x1[:], scr["x1"].rearrange("b p n h -> p b n h")).then_inc(x1_in, 16)
                load(1, 1)
                with sp.Fori(1, GR // 2) as i:
                    for k in range(2):
                        load(i * 2 + k, k)
                for b in range(B):
                    sp.wait_ge(y_read, ((GR - 1) * B + b + 1) * ST)
                    sp.dma_start(out[b].rearrange("(n p) h -> p n h", p=P), x1[:, b]).then_inc(out_stored, 16)
                sp.wait_ge(out_stored, B * 16)

            @block.scalar
            def _(act):
                def split_weights(g, k):
                    act.wait_ge(ug_in, (g + 1) * 32)
                    at_least(act, gate_done, (g - 1) * UN)
                    for i in range(2):
                        nc.scalar.activation(ugs[k][:, i, 0], ugr[:, i], ACT.Copy).then_inc(ug_hi, 1)

                def group(g, k, final):
                    act.wait_ge(wd_in[k], (g - k) * 16 + 32)
                    for u in range(UN):
                        n = g * UN + u
                        if u == 2 and not final:
                            split_weights(g + 1, 1 - k)
                        act.wait_ge(gate_done, n + 1)
                        at_least(act, hf_done, n - 1)
                        nc.scalar.activation(silu[u % 2][:], gp[u % 2][:], ACT.Silu,
                                             scale=scale[k][:, 1, u % IC:u % IC + 1]).then_inc(silu_done, 1)
                        act.wait_ge(hf_done, n + 1)
                        at_least(act, down_done, n - 1)
                        nc.scalar.activation(hs[u % 2][:, 0], hf[u % 2][:], ACT.Copy).then_inc(h_hi, 1)

                split_weights(0, 0)
                in_pairs(act, group)

            @block.vector
            def _(dve):
                def split_weights(g, k):
                    dve.wait_ge(ug_hi, (g + 1) * 2)
                    for i in range(2):
                        nc.vector.tensor_tensor(ugs[k][:, i, 1], ugr[:, i], ugs[k][:, i, 0].bitcast(F32),
                                                ALU.subtract).then_inc(ug_lo, 1)

                def accumulate(g, b):
                    dve.wait_ge(down_done, (g * B + b + 1) * IC)
                    if isinstance(g, int) and g == 0:
                        if b == 0:
                            dve.wait_ge(x1_in, 16)
                    else:
                        dve.wait_ge(y_read, ((g - 1) * B + b + 1) * ST)
                    for j in range(ST):
                        nc.vector.tensor_tensor(x1[:, b, j], yp[j][:], x1[:, b, j], ALU.add).then_inc(y_read, 1)

                def group(g, k, final):
                    dve.wait_ge(wd_in[k], (g - k) * 16 + 32)
                    for u in range(UN):
                        n = g * UN + u
                        if u == 2 and not final:
                            split_weights(g + 1, 1 - k)
                        dve.wait_ge(silu_done, n + 1)
                        at_least(dve, h_hi, n - 1)
                        nc.vector.scalar_tensor_tensor(hf[u % 2][:], up[u % 2][:], scale[k][:, 0, u % IC:u % IC + 1],
                                                       silu[u % 2][:], ALU.mult, ALU.mult).then_inc(hf_done, 1)
                        dve.wait_ge(h_hi, n + 1)
                        nc.vector.tensor_tensor(hs[u % 2][:, 1], hf[u % 2][:], hs[u % 2][:, 0].bitcast(F32),
                                                ALU.subtract).then_inc(h_lo, 1)
                        if u % IC == 0:
                            if u:
                                accumulate(g, u // IC - 1)
                            elif not (isinstance(g, int) and g == 0):
                                accumulate(g - 1, B - 1)

                split_weights(0, 0)
                in_pairs(dve, group)
                accumulate(GR - 1, B - 1)

            @block.tensor
            def _(pe):
                def gate_up(g, k, u):
                    b, i = u // IC, u % IC
                    if isinstance(g, int) and g == 0 and i == 0:
                        pe.wait_ge(xs_in[b], 16)
                    if u == 0:
                        pe.wait_ge(ug_lo, (g + 1) * 2)
                    at_least(pe, hf_done, g * UN + u - 1)
                    for w, acc in ((0, up), (1, gp)):
                        last = split_product(nc, acc[u % 2][:], lambda t, c: ugs[k][:, w, t, c, i * P:(i + 1) * P],
                                             lambda t, c: xs[:, t, b, c])
                    last.then_inc(gate_done, 1)

                def down(g, k, u):
                    b, i = u // IC, u % IC
                    if u == 0:
                        pe.wait_ge(wd_in[k], (g - k) * 16 + 32)
                    if i == 0:
                        at_least(pe, y_read, (g * B + b) * ST)
                    pe.wait_ge(h_lo, g * UN + u + 1)
                    for j in range(ST):
                        last = split_product(nc, yp[j][:], lambda t, c: hs[u % 2][:, t, j * P:(j + 1) * P],
                                             lambda t, c: wds[k][:, i, t], chunks=1, first=i == 0, final=i == IC - 1)
                    last.then_inc(down_done, 1)

                def group(g, k, final):
                    for u in range(UN):
                        if u + 1 < UN:
                            gate_up(g, k, u + 1)
                        elif not final:
                            gate_up(g + 1, 1 - k, 0)
                        down(g, k, u)

                gate_up(0, 0, 0)
                in_pairs(pe, group)


def build(nc, io, out):
    def scratch(name, shape, dt=F32):
        return nc.dram_tensor(f"scr_{name}", shape, dt).ap()

    scr = {
        "q": scratch("q", [2, B, H, S]),
        "k": scratch("k", [2, B, H, TE]),
        "v": scratch("v", [B, NH, P, TT, 2 * HD + 2]),
        "c": scratch("c", [2, B, H, S]),
        "sum": scratch("sum", [2, B * NH * S]),
        "rec": scratch("rec", [B, NH, S]),
        "x1": scratch("x1", [B, P, ST, H]),
        "xs": scratch("xs", [B, 2, P, HC, S]),
        "wdb": scratch("wdb", [P, INTER // P, H]),
        "wd": scratch("wd", [P, INTER // P, 2, H]),
    }
    for name in ("q", "k", "c"):
        scr[name + "4"] = scr[name].rearrange("z b (h d) s -> z (b h) d s", d=HD)
    scr["v4"] = scr["v"].rearrange("b h p t w -> (b h) p t w")
    scr["sum4"] = scr["sum"].rearrange("z (h s) -> z h s", s=S)
    prepare(nc, io, scr)
    attention(nc, io, scr)
    project(nc, io, scr)
    ffn(nc, io, scr, out)


def hadamard(n):
    h = np.ones((1, 1), np.float32)
    while h.shape[0] < n:
        h = np.block([[h, h], [h, -h]])
    return np.ascontiguousarray(h.astype(np.float32))


def kernel(**inputs):
    import concourse.bacc as bacc
    from concourse.bass_utils import run_bass_kernel_spmd

    a = {k: np.asarray(v) for k, v in inputs.items()}
    def columns(v):
        return v.reshape(-1, P).T

    arrays = {
        "x": a["x"],
        "ctxT": a["ctx_2048"].transpose(0, 2, 1),
        "mask": a["mask_BxS2_ik0"],
        "bq": columns(a["L0_xattn_bq"]), "bk": columns(a["L0_xattn_bk"]), "bv": columns(a["L0_xattn_bv"]),
        "bo": a["L0_xattn_bo"],
        "wqT": a["L0_xattn_Wq"].T, "wkT": a["L0_xattn_Wk"].T, "wvT": a["L0_xattn_Wv"].T, "woT": a["L0_xattn_Wo"].T,
        "gamma": a["L0_xattn_ln_gamma"], "beta": a["L0_xattn_ln_beta"],
        "rs": a["L0_xattn_residual_scale"].reshape(1),
        "su_ug": columns(a["L0_ffn_SU_ug"]), "su_dp": columns(a["L0_ffn_SU_dp"]),
        "ws_ug": columns(a["L0_ffn_Wscale_ug"]).reshape(P, 2, INTER // P), "ws_dp": a["L0_ffn_Wscale_dp"],
        "upT": a["L0_ffn_W_up"].T, "gateT": a["L0_ffn_W_gate"].T, "wdT": a["L0_ffn_W_down"].T,
        "ident": np.eye(P, dtype=np.float32), "had": hadamard(P),
    }
    arrays = {f"in_{k}": np.ascontiguousarray(v) for k, v in arrays.items()}
    nc = bacc.Bacc("TRN2", target_bir_lowering=False, num_devices=1)
    io = {k[3:]: nc.dram_tensor(k, v.shape, mybir.dt.from_np(v.dtype), kind="ExternalInput").ap()
          for k, v in arrays.items()}
    out = nc.dram_tensor("out", (B, S, H), F32, kind="ExternalOutput").ap()
    build(nc, io, out)
    r = run_bass_kernel_spmd(nc, [arrays], core_ids=[0])
    return r.results[0]["out"]
```

```python
import numpy as np
import concourse.bass as bass
from concourse import mybir
from contextlib import ExitStack

F32 = mybir.dt.float32
F32R = mybir.dt.float32r
I32 = mybir.dt.int32
ALU = mybir.AluOpType
ACT = mybir.ActivationFunctionType

B, S, H, T = 4, 512, 512, 1601
NH = 16
HD = H // NH
INTER = 2048
P = 128
HC = H // P
ST = S // P
TT = -(-T // P)
TLAST = T - (TT - 1) * P
TE = T + T % 2
TP = TT * P
LOW = float(np.float32(np.exp(-50.0)))
HIGH = float(np.float32(np.exp(50.0)))
EPS = 1e-5
PAIRS = B * NH // 2


class Mem:

    def __init__(self, nc, stack, prefix):
        self.nc, self.stack, self.prefix = nc, stack, prefix

    def sb(self, name, shape, dt=F32):
        return self.stack.enter_context(self.nc.sbuf_tensor(f"{self.prefix}_{name}", shape, dt))

    def ps(self, name, shape, dt=F32):
        return self.stack.enter_context(self.nc.psum_tensor(f"{self.prefix}_{name}", shape, dt))

    def sem(self, name):
        return self.stack.enter_context(self.nc.semaphore(f"{self.prefix}_{name}"))

    def sems(self, name, n):
        return [self.sem(f"{name}{i}") for i in range(n)]


NORM_STEPS = ST + 11


def moments_sum(nc, dve, step, base, ve_done, m):
    v = nc.vector
    st = m.stats[:].rearrange("p j (o k) -> p k o j", o=2)
    mean, m2 = st[:, 1], st[:, 2]
    dve.wait_ge(step, base + ST)
    v.tensor_tensor(m.mean[:], mean[:, 0], mean[:, 1], ALU.add).then_inc(step, 1)
    v.tensor_tensor(m.diff[:], mean[:, 0], mean[:, 1], ALU.subtract).then_inc(step, 1)
    v.tensor_tensor(m.ve[:], m2[:, 0], m2[:, 1], ALU.add).then_inc(step, 1)
    dve.wait_ge(step, base + ST + 3)
    v.tensor_scalar(m.mean[:], m.mean[:], 0.5, None, ALU.mult).then_inc(step, 1)
    v.scalar_tensor_tensor(m.diff[:], m.diff[:], 0.25, m.diff[:], ALU.mult, ALU.mult).then_inc(step, 1)
    v.tensor_scalar(m.ve[:], m.ve[:], 1.0 / H, EPS, ALU.mult, ALU.add).then_inc(step, 1)
    dve.wait_ge(step, base + ST + 6)
    v.tensor_tensor(m.ve[:], m.ve[:], m.diff[:], ALU.add).then_inc(ve_done, 1)


def moments_root(nc, dve, step, base, root_done, call, m):
    v = nc.vector
    dve.wait_ge(root_done, call + 1)
    v.reciprocal(m.inv[:], m.root[:]).then_inc(step, 1)
    dve.wait_ge(step, base + ST + 7)
    v.tensor_tensor(m.tmp[:], m.inv[:], m.inv[:], ALU.mult).then_inc(step, 1)
    dve.wait_ge(step, base + ST + 8)
    v.tensor_tensor(m.tmp[:], m.tmp[:], m.ve[:], ALU.mult).then_inc(step, 1)
    dve.wait_ge(step, base + ST + 9)
    v.tensor_scalar(m.tmp[:], m.tmp[:], -0.5, 1.5, ALU.mult, ALU.add).then_inc(step, 1)
    dve.wait_ge(step, base + ST + 10)
    v.tensor_tensor(m.inv[:], m.inv[:], m.tmp[:], ALU.mult).then_inc(step, 1)
    dve.wait_ge(step, base + ST + 11)


class Moments:

    def __init__(self, m):
        self.stats = m.sb("stats", [P, ST, 6])
        self.mean, self.diff, self.ve, self.root, self.inv, self.tmp = (
            m.sb(n, [P, ST]) for n in ("mean", "diff", "ve", "root", "inv", "tmp"))


def bcast(vec, n):
    return vec.rearrange("(o n) -> o n", o=1).to_broadcast([P, n])


def at_least(eng, sem, value):
    if not (isinstance(value, int) and value <= 0):
        eng.wait_ge(sem, value)


def split_product(nc, out, stationary, moving, chunks=HC, first=True, final=True):
    parts = [(c, a, z) for c in range(chunks) for a, z in ((0, 0), (0, 1), (1, 0))]
    for n, (c, a, z) in enumerate(parts):
        last = nc.tensor.matmul(out, stationary(a, c), moving(z, c),
                                start=first and n == 0, stop=final and n == len(parts) - 1)
    return last


def prepare(nc, io, scr):
    TILES = [3, 3, 3, TT - 9]
    FROM = [0, 3, 6, 9]
    WIDTH = [3 * P, 3 * P, 3 * P, TE - 9 * P]
    WMAX = max(WIDTH)
    NP = len(TILES)
    NORM, TRANS, QUERY = 1, 2, 3
    CONTEXT_AT = [1, 2, 3, 1]
    VD = 2 * HD + 2
    with ExitStack() as stack:
        m = Mem(nc, stack, "pp")
        ident = m.sb("ident", [P, P])
        wraw = [m.sb(f"wraw{i}", [P, HC, H]) for i in range(2)]
        wk, wv, wq = (m.sb(n, [P, 2, HC, H], F32R) for n in ("wk", "wv", "wq"))
        bk, bq = m.sb("bk", [P, HC]), m.sb("bq", [P, HC])
        raw = [m.sb(f"raw{i}", [P, HC, WMAX]) for i in range(2)]
        cs = [m.sb(f"cs{i}", [P, 2, HC, WMAX], F32R) for i in range(2)]
        kf = m.sb("kf", [P, HC, WMAX])
        ks = m.sb("ks", [P, 2, HC, WMAX], F32R)
        vf = [m.sb(f"vf{i}", [P, NH, HD]) for i in range(2)]
        vs = m.sb("vs", [P, NH, 4, VD], F32R)
        maski, maskf = m.sb("maski", [P, TE], I32), m.sb("maskf", [P, TE])
        mcoli, mcol = m.sb("mcoli", [P, TT], I32), m.sb("mcol", [P, TT])
        wcol = m.sb("wcol", [P, TT, 2], F32R)
        ones = m.sb("ones", [P, NH, 4, 2])
        xt = m.sb("xt", [P, ST, H])
        mo = Moments(m)
        xT = m.sb("xT", [P, 2, HC, S], F32R)
        qf = [m.sb(f"qf{i}", [P, S]) for i in range(2)]
        qs = [m.sb(f"qs{i}", [P, 2, S], F32R) for i in range(2)]
        kp = [m.ps(f"kp{i}", [P, WMAX]) for i in range(2)]
        vp = [m.ps(f"vp{i}", [P, NH, HD]) for i in range(2)]
        tp = [m.ps(f"tp{i}", [P, HC, P]) for i in range(2)]
        qp = [m.ps(f"qp{i}", [P, S]) for i in range(2)]

        consts_in, pads = m.sem("consts_in"), m.sem("pads")
        w_in, w_hi, w_lo = m.sems("w_in", 3), m.sem("w_hi"), m.sem("w_lo")
        raw_in = m.sems("raw_in", 2)
        mask_in, mask_done, weight_step, weight_done, wcol_done, wcopy_done = (m.sem(n) for n in (
            "mask_in", "mask_done", "weight_step", "weight_done", "wcol_done", "wcopy_done"))
        c_hi, c_lo = m.sem("c_hi"), m.sem("c_lo")
        k_done, kf_done, k_hi, k_lo, k_stored = (m.sem(n) for n in ("k_done", "kf_done", "k_hi", "k_lo", "k_stored"))
        v_done, vf_done, v_hi, v_lo, v_stored = (m.sem(n) for n in ("v_done", "vf_done", "v_hi", "v_lo", "v_stored"))
        x_in, norm_step, ve_done, root_done, xn_done, t_done, x_hi, x_lo = (m.sem(n) for n in (
            "x_in", "norm_step", "ve_done", "root_done", "xn_done", "t_done", "x_hi", "x_lo"))
        q_done, qf_done, q_hi, q_lo = (m.sem(n) for n in ("q_done", "qf_done", "q_hi", "q_lo"))
        q_stored = m.sems("q_stored", 2)
        V_DMAS = 6

        def over_batches(eng, batch):
            batch(0, False)
            with eng.Fori(1, B - 1) as b:
                batch(b, False)
            batch(B - 1, True)

        with nc.Block() as block:
            @block.sync
            def _(sp):
                def weights(i, w):
                    sp.dma_start(wraw[i % 2][:], io[w].rearrange("(c p) n -> p c n", p=P)).then_inc(w_in[i], 16)

                def context(b, p):
                    t0 = FROM[p] * P
                    w = min(T - t0, WIDTH[p])
                    sp.dma_start(raw[p % 2][:, :, 0:w],
                                 io["ctxT"][b, :, t0:t0 + w].rearrange("(c p) t -> p c t", p=P)).then_inc(raw_in[p % 2], 16)

                def masks(b):
                    sp.wait_ge(mask_done, b)
                    sp.wait_ge(weight_step, b)
                    row = io["mask"][b].rearrange("(o t) -> o t", o=1)
                    sp.dma_start(maski[:, 0:T], row.to_broadcast([P, T])).then_inc(mask_in, 16)
                    sp.dma_start(mcoli[:, 0:TT - 1], io["mask"][b, 0:(TT - 1) * P].rearrange("(n p) -> p n", p=P),
                                 allow_slow_non_contiguous=True).then_inc(mask_in, 16)
                    sp.dma_start(mcoli[0:TLAST, TT - 1:TT], io["mask"][b, (TT - 1) * P:T].rearrange("(p o) -> p o", o=1),
                                 allow_slow_non_contiguous=True).then_inc(mask_in, 16)

                def rows(b):
                    at_least(sp, t_done, b * ST)
                    sp.dma_start(xt[:], io["x"][b].rearrange("(n p) h -> p n h", p=P)).then_inc(x_in, 16)

                def batch(b, final):
                    for p in range(NP):
                        sp.wait_ge(c_lo, b * NP + p)
                        if p + 1 < NP:
                            context(b, p + 1)
                        elif not final:
                            context(b + 1, 0)
                            masks(b + 1)
                            rows(b + 1)

                context(0, 0)
                weights(0, "wkT")
                for t, src in ((bk, "bk"), (bq, "bq"), (ident, "ident")):
                    sp.dma_start(t[:], io[src]).then_inc(consts_in, 16)
                sp.wait_ge(pads, 4)
                masks(0)
                weights(1, "wvT")
                rows(0)
                over_batches(sp, batch)

            @block.gpsimd
            def _(pool):
                nc.gpsimd.memset(maski[:, T - 1:TE], 0).then_inc(pads, 1)
                nc.gpsimd.memset(mcoli[:], 0).then_inc(pads, 1)
                nc.gpsimd.memset(ones[:], 1.0).then_inc(pads, 1)
                nc.gpsimd.memset(raw[(NP - 1) % 2][:, :, WMAX - 1:WMAX], 0.0).then_inc(pads, 1)
                pool.wait_ge(w_lo, 1)
                pool.wait_ge(w_in[1], 16)
                pool.dma_start(wraw[0][:], io["wqT"].rearrange("(c p) n -> p c n", p=P)).then_inc(w_in[2], 16)

                def batch(b, final):
                    for p in range(NP):
                        n, t = TILES[p], FROM[p]
                        if p == 0:
                            pool.wait_ge(wcol_done, 2 * b + 2)
                            pool.wait_ge(pads, 4)
                        at_least(pool, v_stored, (b * V_DMAS + p) * 16)
                        both = wcol[:, t:t + n].bitcast(F32).unsqueeze(1).to_broadcast([P, NH, n, 2])
                        nc.gpsimd.tensor_tensor(vs[:, :, 0:n, 2 * HD:VD], both, ones[:, :, 0:n], ALU.mult).then_inc(wcopy_done, 1)
                        pool.wait_ge(wcopy_done, b * NP + p + 1)
                        dst = scr["v"][b].rearrange("h p t w -> p h t w")
                        for lo, hi in ((0, n),) if p < NP - 1 else ((0, n - 2), (n - 2, n - 1)):
                            pool.wait_ge(v_lo, b * TT + t + hi)
                            pool.dma_start(dst[:, :, t + lo:t + hi], vs[:, :, lo:hi].bitcast(F32)).then_inc(v_stored, 16)
                        if p == NP - 1:
                            pool.wait_ge(v_lo, b * TT + TT)
                            pool.dma_start(dst[0:TLAST, :, TT - 1], vs[0:TLAST, :, n - 1].bitcast(F32)).then_inc(v_stored, 16)
                over_batches(pool, batch)
                pool.wait_ge(v_stored, B * V_DMAS * 16)

            @block.scalar
            def _(act):
                def weights(i, w):
                    act.wait_ge(w_in[i], 16)
                    nc.scalar.activation(w[:, 0], wraw[i % 2][:], ACT.Copy).then_inc(w_hi, 1)

                def context(b, p):
                    w = WIDTH[p]
                    act.wait_ge(raw_in[p % 2], b * (NP // 2 * 16) + (p // 2 + 1) * 16)
                    nc.scalar.activation(cs[p % 2][:, 0, :, 0:w], raw[p % 2][:, :, 0:w], ACT.Copy).then_inc(c_hi, 1)

                def batch(b, final):
                    for p in range(NP):
                        w = WIDTH[p]
                        for k in range(HC):
                            act.wait_ge(kf_done, (b * NP + p) * HC + k + 1)
                            if k == 0:
                                at_least(act, k_stored, (b * NP + p) * 32)
                            nc.scalar.activation(ks[:, 0, k, 0:w], kf[:, k, 0:w], ACT.Copy).then_inc(k_hi, 1)
                            if isinstance(b, int) and b == 0 and p == 0 and k == 0:
                                weights(1, wv)
                            if k == CONTEXT_AT[p]:
                                if p + 1 < NP:
                                    context(b, p + 1)
                                elif not final:
                                    context(b + 1, 0)
                            if p == NORM and k == 2:
                                act.wait_ge(ve_done, b + 1)
                                nc.scalar.activation(mo.root[:], mo.ve[:], ACT.Sqrt).then_inc(root_done, 1)
                            if p == TRANS:
                                act.wait_ge(t_done, b * ST + k + 1)
                                if k == 0:
                                    at_least(act, q_done, b * HC)
                                nc.scalar.activation(xT[:, 0, :, k * P:(k + 1) * P], tp[k % 2][:], ACT.Copy).then_inc(x_hi, 1)
                            if p == QUERY:
                                act.wait_ge(qf_done, b * HC + k + 1)
                                act.wait_ge(q_stored[k % 2], (b * 2 + k // 2) * 32)
                                nc.scalar.activation(qs[k % 2][:, 0], qf[k % 2][:], ACT.Copy).then_inc(q_hi, 1)
                                act.wait_ge(q_hi, b * HC + k + 1)
                                act.wait_ge(q_lo, b * HC + k + 1)
                                for half in range(2):
                                    act.dma_start(scr["q"][half, b, k * P:(k + 1) * P], qs[k % 2][:, half].bitcast(F32)
                                                  ).then_inc(q_stored[k % 2], 16)
                        if isinstance(b, int) and b == 0 and p == 1:
                            weights(2, wq)
                        if p == 0:
                            act.wait_ge(weight_done, b + 1)
                        for n in range(TILES[p]):
                            t = FROM[p] + n
                            i = b * TT + t
                            act.wait_ge(v_done, i + 1)
                            act.wait_ge(v_lo, i - 1 if t else i)
                            rows = TLAST if t == TT - 1 else P
                            nc.scalar.activation(vf[t % 2][0:rows], vp[t % 2][0:rows], ACT.Copy,
                                                 scale=mcol[0:rows, t:t + 1]).then_inc(vf_done, 1)
                            if n == 0:
                                at_least(act, v_stored, (b * V_DMAS + p) * 16)
                            act.wait_ge(vf_done, i + 1)
                            nc.scalar.activation(vs[0:rows, :, n, 0:HD], vf[t % 2][0:rows], ACT.Copy).then_inc(v_hi, 1)
                            if n == 0:
                                act.wait_ge(k_hi, (b * NP + p) * HC + HC)
                                act.wait_ge(k_lo, (b * NP + p) * HC + HC)
                                t0 = FROM[p] * P
                                for half in range(2):
                                    act.dma_start(scr["k"][half, b, :, t0:t0 + w].rearrange("(c p) t -> p c t", p=P),
                                                  ks[:, half, :, 0:w].bitcast(F32)).then_inc(k_stored, 16)

                context(0, 0)
                weights(0, wk)
                over_batches(act, batch)
                act.wait_ge(k_stored, B * NP * 32)
                for i in range(2):
                    act.wait_ge(q_stored[i], B * 64)

            @block.vector
            def _(dve):
                def weights(i, w):
                    dve.wait_ge(w_hi, i + 1)
                    nc.vector.tensor_tensor(w[:, 1], wraw[i % 2][:], w[:, 0].bitcast(F32), ALU.subtract).then_inc(w_lo, 1)

                def context(b, p):
                    w = WIDTH[p]
                    dve.wait_ge(c_hi, b * NP + p + 1)
                    nc.vector.tensor_tensor(cs[p % 2][:, 1, :, 0:w], raw[p % 2][:, :, 0:w],
                                            cs[p % 2][:, 0, :, 0:w].bitcast(F32), ALU.subtract).then_inc(c_lo, 1)

                def masks(b):
                    dve.wait_ge(mask_in, b * 48 + 48)
                    nc.vector.tensor_scalar(maskf[:], maski[:], 0.5, None, ALU.is_gt).then_inc(mask_done, 1)
                    at_least(dve, vf_done, b * TT)
                    at_least(dve, wcopy_done, b * NP)
                    nc.vector.tensor_scalar(mcol[:], mcoli[:], 0.5, None, ALU.is_gt).then_inc(weight_step, 1)
                    dve.wait_ge(weight_step, b + 1)
                    nc.vector.tensor_scalar(mcol[:], mcol[:], 1.0 - LOW, LOW, ALU.mult, ALU.add).then_inc(weight_done, 1)
                    dve.wait_ge(weight_done, b + 1)
                    nc.vector.tensor_copy(wcol[:, :, 0], mcol[:]).then_inc(wcol_done, 1)
                    dve.wait_ge(wcol_done, 2 * b + 1)
                    nc.vector.tensor_tensor(wcol[:, :, 1], mcol[:], wcol[:, :, 0].bitcast(F32), ALU.subtract).then_inc(wcol_done, 1)
                    dve.wait_ge(mask_done, b + 1)

                def key_lo(b, p, k):
                    w = WIDTH[p]
                    dve.wait_ge(k_hi, (b * NP + p) * HC + k + 1)
                    nc.vector.tensor_tensor(ks[:, 1, k, 0:w], kf[:, k, 0:w], ks[:, 0, k, 0:w].bitcast(F32),
                                            ALU.subtract).then_inc(k_lo, 1)

                def batch(b, final):
                    masks(b)
                    for p in range(NP):
                        w = WIDTH[p]
                        for k in range(HC):
                            dve.wait_ge(k_done, (b * NP + p) * HC + k + 1)
                            nc.vector.scalar_tensor_tensor(kf[:, k, 0:w], kp[k % 2][:, 0:w], bk[:, k:k + 1],
                                                           maskf[:, FROM[p] * P:FROM[p] * P + w],
                                                           ALU.add, ALU.mult).then_inc(kf_done, 1)
                            if k:
                                key_lo(b, p, k - 1)
                            if isinstance(b, int) and b == 0 and p == 0 and k == 0:
                                weights(1, wv)
                            if k == CONTEXT_AT[p]:
                                if p + 1 < NP:
                                    context(b, p + 1)
                                elif not final:
                                    context(b + 1, 0)
                            if p == NORM:
                                if k < 2:
                                    dve.wait_ge(x_in, b * 16 + 16)
                                    for j in (2 * k, 2 * k + 1):
                                        nc.vector.bn_stats(mo.stats[:, j], xt[:, j]).then_inc(norm_step, 1)
                                if k == 1:
                                    moments_sum(nc, dve, norm_step, b * NORM_STEPS, ve_done, mo)
                                if k == 2:
                                    moments_root(nc, dve, norm_step, b * NORM_STEPS, root_done, b, mo)
                                if k == 3:
                                    for j in range(ST):
                                        nc.vector.tensor_scalar(xt[:, j], xt[:, j], mo.mean[:, j:j + 1], mo.inv[:, j:j + 1],
                                                                ALU.subtract, ALU.mult).then_inc(xn_done, 1)
                            if p == TRANS:
                                dve.wait_ge(x_hi, b * ST + k + 1)
                                cols = slice(k * P, (k + 1) * P)
                                nc.vector.tensor_tensor(xT[:, 1, :, cols], tp[k % 2][:], xT[:, 0, :, cols].bitcast(F32),
                                                        ALU.subtract).then_inc(x_lo, 1)
                            if p == QUERY:
                                dve.wait_ge(q_done, b * HC + k + 1)
                                dve.wait_ge(q_lo, b * HC + k - 1 if k else b * HC)
                                nc.vector.tensor_scalar(qf[k % 2][:], qp[k % 2][:], bq[:, k:k + 1], None, ALU.add).then_inc(qf_done, 1)
                                dve.wait_ge(q_hi, b * HC + k + 1)
                                nc.vector.tensor_tensor(qs[k % 2][:, 1], qf[k % 2][:], qs[k % 2][:, 0].bitcast(F32),
                                                        ALU.subtract).then_inc(q_lo, 1)
                        key_lo(b, p, HC - 1)
                        if isinstance(b, int) and b == 0 and p == 1:
                            weights(2, wq)
                        for n in range(TILES[p]):
                            t = FROM[p] + n
                            rows = TLAST if t == TT - 1 else P
                            dve.wait_ge(v_hi, b * TT + t + 1)
                            nc.vector.tensor_tensor(vs[0:rows, :, n, HD:2 * HD], vf[t % 2][0:rows],
                                                    vs[0:rows, :, n, 0:HD].bitcast(F32), ALU.subtract).then_inc(v_lo, 1)

                context(0, 0)
                weights(0, wk)
                dve.wait_ge(consts_in, 16 * 3)
                over_batches(dve, batch)

            @block.tensor
            def _(pe):
                def batch(b, final):
                    for p in range(NP):
                        w = WIDTH[p]
                        c0 = cs[p % 2]
                        pe.wait_ge(c_lo, b * NP + p + 1)
                        for k in range(HC):
                            i = p * HC + k
                            pe.wait_ge(kf_done, b * NP * HC + (i - 1 if i else 0))
                            split_product(nc, kp[k % 2][:, 0:w], lambda t, c: wk[:, t, c, k * P:(k + 1) * P],
                                          lambda t, c: c0[:, t, c, 0:w]).then_inc(k_done, 1)
                            if p == TRANS:
                                if k == 0:
                                    pe.wait_ge(xn_done, b * ST + ST)
                                pe.wait_ge(x_lo, b * ST + (k - 1 if k else 0))
                                for c in range(HC):
                                    last = nc.tensor.transpose(tp[k % 2][:, c], xt[:, k, c * P:(c + 1) * P], ident[:])
                                last.then_inc(t_done, 1)
                            if p == QUERY:
                                if k == 0:
                                    pe.wait_ge(w_lo, 3)
                                    pe.wait_ge(x_lo, b * ST + ST)
                                pe.wait_ge(qf_done, b * HC + (k - 1 if k else 0))
                                split_product(nc, qp[k % 2][:], lambda t, c: wq[:, t, c, k * P:(k + 1) * P],
                                              lambda t, c: xT[:, t, c, :]).then_inc(q_done, 1)
                        if p == 0:
                            pe.wait_ge(w_lo, 2)
                        for n in range(TILES[p]):
                            t = FROM[p] + n
                            rows = TLAST if t == TT - 1 else P
                            pe.wait_ge(vf_done, b * TT + (t - 1 if t else 0))
                            split_product(nc, vp[t % 2][0:rows], lambda z, c: c0[:, z, c, n * P:n * P + rows],
                                          lambda z, c: wv[:, z, c, :]).then_inc(v_done, 1)

                pe.wait_ge(w_lo, 1)
                pe.wait_ge(consts_in, 16 * 3)
                over_batches(pe, batch)


class Early:

    CONSTS = 9

    def __init__(self, m):
        self.block = m.sb("block", [P, 4 * HC * H])
        self.ca, self.cb, self.rb, self.wraw = (
            self.block[:, i * HC * H:(i + 1) * HC * H].rearrange("p (c h) -> p c h", c=HC) for i in range(4))
        self.ident = m.sb("ident", [P, P])
        self.had = m.sb("had", [P, 2, P])
        self.bv, self.su, self.rs = m.sb("bv", [P, HC]), m.sb("su", [P, HC]), m.sb("rs", [P, 1])
        self.bo, self.gamma, self.beta, self.wsc = (m.sb(n, [P, H]) for n in ("bo", "gamma", "beta", "wsc"))

    def load_consts(self, eng, io, done):
        for t, src in ((self.ident[:], io["ident"]), (self.had[:, 0], io["had"]), (self.bv[:], io["bv"]),
                       (self.su[:], io["su_ug"]), (self.rs[:], bcast(io["rs"], 1)), (self.bo[:], bcast(io["bo"], H)),
                       (self.gamma[:], bcast(io["gamma"], H)), (self.beta[:], bcast(io["beta"], H)),
                       (self.wsc[:], bcast(io["ws_dp"], H))):
            eng.dma_start(t, src).then_inc(done, 16)


def load_recips(eng, scr, rb, b, done):
    for c in range(HC):
        src = scr["rec"][b, 4 * c:4 * c + 4].unsqueeze(1).to_broadcast([4, HD, S])
        eng.dma_start(rb[:, c], src).then_inc(done, 16)


def attention(nc, io, scr, early):
    GROUPS = [3, 2, 3, 3, 2]
    FROM = [0, 3, 5, 8, 11]
    SPLIT = [True, False, True, True, False]
    NG = len(GROUPS)
    PG = 2 * NG
    GMAX = max(GROUPS)
    NSC = 2
    AHEAD = NG + 1
    UNROLL = 3
    FULL = TT - 1
    SCALE = 1.0 / float(np.sqrt(HD))
    VD = 2 * HD + 2
    SLOT = {g: i for i, g in enumerate(g for g in range(PG) if SPLIT[g % NG])}
    with ExitStack() as stack:
        m = Mem(nc, stack, "at")
        kst = [m.sb(f"kst{j}", [P, TP], F32R) for j in range(2)]
        qst = [m.sb(f"qst{j}", [P, S], F32R) for j in range(2)]
        vst = [m.sb(f"vst{j}", [P, TT, VD], F32R) for j in range(2)]
        probs = [m.sb(f"probs{i}", [P, GROUPS[i % NG], S]) for i in range(PG)]
        parts = [m.sb(f"parts{i}", [P, 2, GMAX, S], F32R) for i in range(len(SLOT))]
        ob = [m.sb(f"ob{j}", [VD, S]) for j in range(2)]
        sc = [m.ps(f"sc{i}", [P, GMAX, S]) for i in range(NSC)]
        acc = [m.ps(f"acc{j}", [VD, S]) for j in range(2)]

        pads = m.sem("pads")
        kq_in, v_in = m.sems("kq_in", 2), m.sems("v_in", 2)
        scores_done, values_done = m.sems("scores_done", 2), m.sems("values_done", 2)
        exp_done, clip_done, p_hi, p_lo = (m.sem(n) for n in ("exp_done", "clip_done", "p_hi", "p_lo"))
        acc_read, stored = m.sems("acc_read", 2), m.sems("stored", 2)
        fly_in, fly, fly_out = (m.sem(n) for n in ("fly_in", "fly", "fly_out"))
        NS = len(SLOT)
        IC = INTER // P
        STAGES = IC.bit_length() - 1
        half_block = IC * H // 2
        wd = [early.block[:, i * half_block:(i + 1) * half_block].rearrange("p (c n) -> p c n", c=IC) for i in range(2)]
        S0 = NH * S // P
        sums0, recip0 = m.sb("sums0", [P, 2, S0]), m.sb("recip0", [P, S0])
        early_in, sum_in, rec_step, rec_out, r_in, ab_done, c_done = (m.sem(n) for n in (
            "early_in", "sum_in", "rec_step", "rec_out", "r_in", "ab_done", "c_done"))

        with nc.Block() as block:
            @block.sync
            def _(sp):
                def keys(n, j):
                    h = n * 2 + j
                    at_least(sp, scores_done[j], n * NG)
                    for i in range(2):
                        rows = slice(i * 2 * HD, (i + 1) * 2 * HD)
                        sp.dma_start(kst[j][rows, 0:TE].bitcast(F32), scr["k4"][:, h]).then_inc(kq_in[j], 16)
                        sp.dma_start(qst[j][rows].bitcast(F32), scr["q4"][i, h].unsqueeze(0).to_broadcast([2, HD, S])
                                     ).then_inc(kq_in[j], 16)

                def weighted_values(n, j):
                    h = n * 2 + j
                    at_least(sp, values_done[j], n * NG)
                    sp.dma_start(vst[j][:, 0:FULL].bitcast(F32), scr["v4"][h, :, 0:FULL]).then_inc(v_in[j], 16)
                    sp.dma_start(vst[j][0:TLAST, FULL].bitcast(F32), scr["v4"][h, 0:TLAST, FULL]).then_inc(v_in[j], 16)

                def store(n, j):
                    h = n * 2 + j
                    sp.wait_ge(acc_read[j], n + 1)
                    sp.dma_start(scr["c4"][0, h], ob[j][0:HD]).then_inc(stored[j], 16)
                    sp.dma_start(scr["c4"][1, h], ob[j][HD:2 * HD]).then_inc(stored[j], 16)
                    sp.dma_start(scr["sum4"][:, h], ob[j][2 * HD:VD]).then_inc(stored[j], 16)

                def turn(n, second):
                    keys(n, 0)
                    weighted_values(n - 1, 1)
                    if not second:
                        store(n - 2, 1)
                    keys(n, 1)
                    weighted_values(n, 0)
                    store(n - 1, 0)

                keys(0, 0)
                weighted_values(0, 0)
                keys(0, 1)
                turn(1, True)
                with sp.Fori(2, PAIRS) as n:
                    turn(n, False)
                weighted_values(PAIRS - 1, 1)
                store(PAIRS - 2, 1)
                for j in range(2):
                    store(PAIRS - 1, j)
                for j in range(2):
                    sp.wait_ge(stored[j], 48 * PAIRS)

            @block.gpsimd
            def _(pool):
                for j in range(2):
                    nc.gpsimd.memset(kst[j][:, TE:TP].bitcast(F32), 0.0).then_inc(pads, 1)
                for j in range(2):
                    pool.wait_ge(v_in[j], 32)
                for half in range(2):
                    cols = slice(half * (H // 2), (half + 1) * (H // 2))
                    base = half * 2 * STAGES
                    if half:
                        pool.wait_ge(fly, base)
                        pool.wait_ge(fly_out, 16)
                    pool.dma_start(wd[0], io["wdT"].rearrange("(c p) n -> p c n", p=P)[:, :, cols]).then_inc(fly_in, 16)
                    pool.wait_ge(fly_in, 16 * (half + 1))
                    for s in range(STAGES):
                        src, dst = wd[s % 2], wd[(s + 1) % 2]
                        z = 1 << s
                        si = src.rearrange("p (a two z) n -> p a two (z n)", two=2, z=z)
                        di = dst.rearrange("p (a two z) n -> p a two (z n)", two=2, z=z)
                        if s:
                            pool.wait_ge(fly, base + 2 * s)
                        nc.gpsimd.tensor_tensor(di[:, :, 0], si[:, :, 0], si[:, :, 1], ALU.add).then_inc(fly, 1)
                        nc.gpsimd.tensor_tensor(di[:, :, 1], si[:, :, 0], si[:, :, 1], ALU.subtract).then_inc(fly, 1)
                    pool.wait_ge(fly, base + 2 * STAGES)
                    pool.dma_start(scr["wdb"][:, :, cols], wd[STAGES % 2]).then_inc(fly_out, 16)
                pool.wait_ge(fly_out, 32)
                early.load_consts(pool, io, early_in)
                pool.dma_start(early.wraw, io["woT"].rearrange("(c p) n -> p c n", p=P)).then_inc(early_in, 16)
                for j in range(2):
                    pool.wait_ge(stored[j], 48 * (NH // 2))
                for t, half in ((early.ca, 0), (early.cb, 1)):
                    pool.dma_start(t, scr["c"][half, 0].rearrange("(c p) s -> p c s", p=P)).then_inc(early_in, 16)
                pool.dma_start(sums0[:], scr["sum"][:, 0:NH * S].rearrange("z (p f) -> p z f", p=P)).then_inc(sum_in, 16)
                pool.wait_ge(rec_step, 2)
                pool.dma_start(scr["rec"][0].rearrange("h s -> (h s)").rearrange("(p f) -> p f", p=P), recip0[:]).then_inc(rec_out, 16)
                pool.wait_ge(rec_out, 16)
                load_recips(pool, scr, early.rb, 0, r_in)
                pool.wait_ge(early_in, 16 * (early.CONSTS + 3))
                nc.gpsimd.tensor_tensor(early.ca, early.ca, early.cb, ALU.add).then_inc(ab_done, 1)
                pool.wait_ge(ab_done, 1)
                pool.wait_ge(r_in, 16 * HC)
                nc.gpsimd.tensor_tensor(early.ca, early.ca, early.rb, ALU.mult).then_inc(c_done, 1)

            @block.scalar
            def _(act):
                def exp(n, g):
                    act.wait_ge(scores_done[g // NG], n * NG + g % NG + 1)
                    if g in SLOT:
                        at_least(act, p_lo, (n - 1) * NS + SLOT[g] + 1)
                    else:
                        at_least(act, values_done[g // NG], n * NG)
                    nc.scalar.activation(probs[g][:], sc[g % NSC][:, 0:GROUPS[g % NG]], ACT.Exp, scale=SCALE).then_inc(exp_done, 1)

                def split_hi(n, g):
                    if g in SLOT:
                        act.wait_ge(clip_done, n * PG + g + 1)
                        at_least(act, values_done[g // NG], n * NG)
                        nc.scalar.activation(parts[SLOT[g]][:, 0], probs[g][:], ACT.Copy).then_inc(p_hi, 1)

                def pair(n, first):
                    for g in range(PG):
                        exp(n, g)
                        if g >= 2:
                            split_hi(n, g - 2)
                        elif not first:
                            split_hi(n - 1, g + PG - 2)

                pair(0, True)
                with act.Fori(0, (PAIRS - 1) // UNROLL) as i:
                    for r in range(UNROLL):
                        pair(i * UNROLL + (1 + r), False)
                for n in range(PAIRS - (PAIRS - 1) % UNROLL, PAIRS):
                    pair(n, False)
                for g in (PG - 2, PG - 1):
                    split_hi(PAIRS - 1, g)

            @block.vector
            def _(dve):
                def collect(n, j):
                    dve.wait_ge(values_done[j], (n + 1) * NG)
                    at_least(dve, stored[j], n * 48)
                    nc.vector.tensor_copy(ob[j][:], acc[j][:]).then_inc(acc_read[j], 1)

                def split_lo(n, g):
                    if g in SLOT:
                        part = parts[SLOT[g]]
                        dve.wait_ge(p_hi, n * NS + SLOT[g] + 1)
                        nc.vector.tensor_tensor(part[:, 1], probs[g][:], part[:, 0].bitcast(F32), ALU.subtract).then_inc(p_lo, 1)

                def pair(n, first):
                    for g in range(PG):
                        dve.wait_ge(exp_done, n * PG + g + 1)
                        nc.vector.tensor_scalar(probs[g][:], probs[g][:], LOW, HIGH, ALU.max, ALU.min).then_inc(clip_done, 1)
                        if g >= 2:
                            split_lo(n, g - 2)
                        elif not first:
                            split_lo(n - 1, g + PG - 2)
                        if g == 4 and not first:
                            collect(n - 1, 1)
                        if g == NG + 4:
                            collect(n, 0)

                pair(0, True)
                pair(1, False)
                with dve.Fori(2, PAIRS - 1) as n:
                    pair(n, False)
                dve.wait_ge(sum_in, 16)
                nc.vector.tensor_tensor(sums0[:, 0], sums0[:, 0], sums0[:, 1], ALU.add).then_inc(rec_step, 1)
                dve.wait_ge(rec_step, 1)
                nc.vector.reciprocal(recip0[:], sums0[:, 0]).then_inc(rec_step, 1)
                pair(PAIRS - 1, False)
                for g in (PG - 2, PG - 1):
                    split_lo(PAIRS - 1, g)
                collect(PAIRS - 1, 1)

            @block.tensor
            def _(pe):
                def scores(n, g):
                    j, k = g // NG, g % NG
                    if k == 0:
                        pe.wait_ge(kq_in[j], (n + 1) * 64)
                    at_least(pe, exp_done, n * PG + g - NSC + 1)
                    for i in range(GROUPS[k]):
                        t = FROM[k] + i
                        last = nc.tensor.matmul(sc[g % NSC][:, i], kst[j][:, t * P:(t + 1) * P], qst[j][:],
                                                start=True, stop=True)
                    last.then_inc(scores_done[j], 1)

                def values(n, g):
                    j, k = g // NG, g % NG
                    if k == 0:
                        pe.wait_ge(v_in[j], (n + 1) * 32)
                        pe.wait_ge(acc_read[j], n)
                    if g in SLOT:
                        pe.wait_ge(p_lo, n * NS + SLOT[g] + 1)
                    else:
                        pe.wait_ge(clip_done, n * PG + g + 1)
                    for i in range(GROUPS[k]):
                        t = FROM[k] + i
                        rows = TLAST if t == FULL else P
                        weights = vst[j][0:rows, t]
                        if g in SLOT:
                            for z in range(2):
                                last = nc.tensor.matmul(acc[j][:], weights, parts[SLOT[g]][0:rows, z, i],
                                                        start=t == 0 and z == 0, stop=t == FULL and z == 1)
                        else:
                            last = nc.tensor.matmul(acc[j][:], weights.bitcast(F32), probs[g][0:rows, i],
                                                    start=t == 0, stop=t == FULL)
                    last.then_inc(values_done[j], 1)

                def pair(n, final):
                    for g in range(PG):
                        if g + AHEAD < PG:
                            scores(n, g + AHEAD)
                        elif not final:
                            scores(n + 1, g + AHEAD - PG)
                        values(n, g)

                pe.wait_ge(pads, 2)
                for g in range(AHEAD):
                    scores(0, g)
                pair(0, False)
                with pe.Fori(1, PAIRS - 1) as n:
                    pair(n, False)
                pair(PAIRS - 1, True)


GC = 2


class Handover:

    def __init__(self, m):
        self.xs = m.sb("xs", [P, 2, HC, S], F32R)
        self.x1 = m.sb("x1", [P, ST, H])
        self.ugr = m.sb("ugr", [P, 2, HC, GC * P])
        self.ugs0 = m.sb("ugs0", [P, 2, 2, HC, GC * P], F32R)


def load_up_gate(sp, io, ugr, g, done):
    for i, w in enumerate(("upT", "gateT")):
        src = io[w].rearrange("(c p) n -> p c n", p=P)
        sp.dma_start(ugr[:, i], src[:, :, bass.ds(g * GC * P, GC * P)]).then_inc(done, 16)


def project(nc, io, scr, early, hand):
    WC = INTER // P // B
    NOP = ST - 1
    with ExitStack() as stack:
        m = Mem(nc, stack, "pr")
        ident, had, bv, su, rs = early.ident, early.had, early.bv, early.su, early.rs
        bo, gamma, beta, wsc = early.bo, early.gamma, early.beta, early.wsc
        ca, cb, rb, wraw = early.ca, early.cb, early.rb, early.wraw
        xn = wraw
        wo = m.sb("wo", [P, 2, HC, H], F32R)
        bvb = m.sb("bvb", [P, HC, P])
        SUMS = (B - 1) * NH * S // P
        sums, recip = m.sb("sums", [P, 2, SUMS]), m.sb("recip", [P, SUMS])
        cs = m.sb("cs", [P, 2, HC, S], F32R)
        xt, d = m.sb("xt", [P, ST, H]), m.sb("d", [P, ST, H])
        xs, x1, ugr, ugs = hand.xs, hand.x1, hand.ugr, hand.ugs0
        mo = Moments(m)
        xT, xR = m.sb("xT", [P, HC, S]), m.sb("xR", [P, HC, S])
        wd, su_dp = m.sb("wd", [P, WC, H]), m.sb("su_dp", [P, WC])
        wdf = m.sb("wdf", [P, WC, H])
        wds = m.sb("wds", [P, WC, 2, H], F32R)
        op = [m.ps(f"op{j}", [P, H]) for j in range(NOP)]
        wp = m.ps("wp", [P, H])
        tp = [m.ps(f"tp{j}", [P, S]) for j in range(HC)]

        (wd_in, sum_in, rec_out, w_hi, w_lo, bvb_done, bias_done, rs_step, had_done, rec_step, ab_in,
         r_in, x_in, ab_done, c_done, c_hi, c_lo, o_done, d_done, beta_done, norm_step, ve_done, root_done, g_done,
         x1_done, x1_stored, xn_done, t_done, xT_done, fly, rot_done, xs_hi, xs_lo, xs_stored, wrot_done, wdf_done,
         wsc_done, wd_hi, wd_lo, wd_stored, ug_in, ug_hi, ug_lo) = (m.sem(n) for n in (
             "wd_in", "sum_in", "rec_out", "w_hi", "w_lo", "bvb_done", "bias_done", "rs_step",
             "had_done", "rec_step", "ab_in", "r_in", "x_in", "ab_done", "c_done", "c_hi", "c_lo", "o_done", "d_done",
             "beta_done", "norm_step", "ve_done", "root_done", "g_done", "x1_done", "x1_stored", "xn_done", "t_done",
             "xT_done", "fly", "rot_done", "xs_hi", "xs_lo", "xs_stored", "wrot_done", "wdf_done", "wsc_done",
             "wd_hi", "wd_lo", "wd_stored", "ug_in", "ug_hi", "ug_lo"))

        def over_batches(eng, batch):
            batch(0, True, False)
            batch(1, False, False)
            with eng.Fori(2, B - 1) as b:
                batch(b, False, False)
            batch(B - 1, False, True)

        with nc.Block() as block:
            @block.sync
            def _(sp):
                def heads(b):
                    at_least(sp, c_lo, b * HC)
                    for t, half in ((ca, 0), (cb, 1)):
                        sp.dma_start(t, scr["c"][half, b].rearrange("(c p) s -> p c s", p=P)).then_inc(ab_in, 16)
                    load_recips(sp, scr, rb, b, r_in)

                def rows(b):
                    at_least(sp, x1_done, b * ST)
                    sp.dma_start(xt[:], io["x"][b].rearrange("(n p) h -> p n h", p=P)).then_inc(x_in, 16)

                def down(b):
                    at_least(sp, wrot_done, b * WC)
                    sp.dma_start(wd[:], scr["wdb"][:, bass.ds(b * WC, WC)]).then_inc(wd_in, 16)
                    at_least(sp, wdf_done, b * WC)
                    sp.dma_start(su_dp[:], io["su_dp"][:, bass.ds(b * WC, WC)]).then_inc(wd_in, 16)

                def store_down(b):
                    sp.wait_ge(wd_lo, b * WC + WC)
                    sp.dma_start(scr["wd"][:, bass.ds(b * WC, WC)], wds[:].bitcast(F32)).then_inc(wd_stored, 16)

                def store_rotated(b):
                    sp.wait_ge(xs_hi, b * HC + HC)
                    sp.wait_ge(xs_lo, b * HC + HC)
                    sp.dma_start(scr["xs"][b].rearrange("t p c s -> p t c s"), xs[:].bitcast(F32)).then_inc(xs_stored, 16)

                def turn(b, loads, heads_too):
                    if heads_too:
                        heads(b + 2)
                    if loads:
                        down(b + 1)
                    if loads:
                        sp.wait_ge(x1_done, b * ST + ST)
                        sp.dma_start(scr["x1"][b], x1[:]).then_inc(x1_stored, 16)
                        rows(b + 1)
                    if not (isinstance(b, int) and b == 0):
                        store_rotated(b - 1)
                    store_down(b)

                sp.dma_start(sums[:], scr["sum"][:, NH * S:B * NH * S].rearrange("z (p f) -> p z f", p=P)).then_inc(sum_in, 16)
                rows(0)
                down(0)
                sp.wait_ge(rec_step, 2)
                sp.dma_start(scr["rec"][1:B].rearrange("b h s -> (b h s)").rearrange("(p f) -> p f", p=P), recip[:]).then_inc(rec_out, 16)
                sp.wait_ge(rec_out, 16)
                heads(1)
                turn(0, True, True)
                with sp.Fori(1, B - 2) as b:
                    turn(b, True, True)
                turn(B - 2, True, False)
                load_up_gate(sp, io, ugr, 0, ug_in)
                turn(B - 1, False, False)
                sp.wait_ge(x1_stored, (B - 1) * 16)
                sp.wait_ge(xs_stored, (B - 1) * 16)
                sp.wait_ge(wd_stored, B * 16)

            @block.gpsimd
            def _(pool):
                def front(b):
                    at_least(pool, ab_in, b * 32)
                    nc.gpsimd.tensor_tensor(ca, ca, cb, ALU.add).then_inc(ab_done, 1)
                    pool.wait_ge(ab_done, b)
                    pool.wait_ge(r_in, b * 16 * HC)
                    nc.gpsimd.tensor_tensor(ca, ca, rb, ALU.mult).then_inc(c_done, 1)

                def rows(b):
                    pool.wait_ge(x_in, b * 16 + 16)
                    nc.gpsimd.tensor_tensor(xt[:], xt[:], beta[:].unsqueeze(1).to_broadcast([P, ST, H]), ALU.add).then_inc(beta_done, 1)

                def turn(b, first, final):
                    if not final:
                        front(b + 1)
                    if not first:
                        rows(b)
                    for i in range(WC):
                        pool.wait_ge(wdf_done, b * WC + i + 1)
                        nc.gpsimd.tensor_tensor(wdf[:, i], wdf[:, i], wsc[:], ALU.mult).then_inc(wsc_done, 1)
                    for i in range(WC):
                        pool.wait_ge(wd_hi, b * WC + i + 1)
                        nc.gpsimd.tensor_tensor(wds[:, i, 1], wdf[:, i], wds[:, i, 0].bitcast(F32), ALU.subtract).then_inc(wd_lo, 1)

                rows(0)
                pool.wait_ge(rs_step, 5)
                over_batches(pool, turn)

            @block.scalar
            def _(act):
                def front_hi(b):
                    act.wait_ge(c_done, b)
                    at_least(act, o_done, b * ST)
                    for c in range(HC):
                        nc.scalar.activation(cs[:, 0, c], ca[:, c], ACT.Copy).then_inc(c_hi, 1)

                def root(b, r):
                    act.wait_ge(ve_done, 2 * b + r + 1)
                    nc.scalar.activation(mo.root[:], mo.ve[:], ACT.Sqrt).then_inc(root_done, 1)

                def signs(b):
                    for c in range(HC):
                        act.wait_ge(t_done, b * HC + c + 1)
                        if c == 0:
                            at_least(act, fly, b * 2)
                        nc.scalar.activation(xT[:, c], tp[c][:], ACT.Copy, scale=su[:, c:c + 1]).then_inc(xT_done, 1)

                def rotated_hi(b):
                    for c in range(HC):
                        act.wait_ge(rot_done, b * HC + c + 1)
                        if c == 0:
                            at_least(act, xs_stored, b * 16)
                        nc.scalar.activation(xs[:, 0, c], tp[c][:], ACT.Copy).then_inc(xs_hi, 1)

                def down(b, chunks):
                    for i in chunks:
                        act.wait_ge(wrot_done, b * WC + i + 1)
                        nc.scalar.activation(wdf[:, i], wp[:], ACT.Copy, scale=su_dp[:, i:i + 1]).then_inc(wdf_done, 1)

                def turn(b, first, final):
                    if not first:
                        signs(b - 1)
                    act.wait_ge(wd_in, b * 32 + 32)
                    at_least(act, wd_lo, b * WC)
                    down(b, range(WC // 2))
                    root(b, 0)
                    if not (first or final):
                        front_hi(b + 1)
                    if not first:
                        rotated_hi(b - 1)
                    down(b, range(WC // 2, WC))
                    if first:
                        front_hi(b + 1)
                    root(b, 1)
                    at_least(act, wd_stored, b * 16)
                    for i in range(WC):
                        act.wait_ge(wsc_done, b * WC + i + 1)
                        nc.scalar.activation(wds[:, i, 0], wdf[:, i], ACT.Copy).then_inc(wd_hi, 1)

                nc.scalar.activation(wo[:, 0], wraw, ACT.Copy).then_inc(w_hi, 1)
                nc.scalar.activation(had[:, 1], had[:, 0], ACT.Copy, scale=-1.0).then_inc(had_done, 1)
                front_hi(0)
                act.wait_ge(rs_step, 5)
                over_batches(act, turn)
                signs(B - 1)
                act.wait_ge(ug_in, 32)
                for i in range(2):
                    nc.scalar.activation(ugs[:, i, 0], ugr[:, i], ACT.Copy).then_inc(ug_hi, 1)
                rotated_hi(B - 1)

            @block.vector
            def _(dve):
                def front_lo(b):
                    for c in range(HC):
                        dve.wait_ge(c_hi, b * HC + c + 1)
                        nc.vector.tensor_tensor(cs[:, 1, c], ca[:, c], cs[:, 0, c].bitcast(F32), ALU.subtract).then_inc(c_lo, 1)

                def delta(b, j):
                    dve.wait_ge(o_done, b * ST + j + 1)
                    nc.vector.scalar_tensor_tensor(d[:, j], op[j % NOP][:], rs[:, 0:1], bo[:], ALU.mult, ALU.add).then_inc(d_done, 1)

                def stats(b, r, j, src, src_done):
                    dve.wait_ge(src_done, b * ST + j + 1)
                    nc.vector.bn_stats(mo.stats[:, j], src[:, j]).then_inc(norm_step, 1)

                def butterfly(b):
                    dve.wait_ge(xT_done, b * HC + HC)
                    at_least(dve, rot_done, b * HC)
                    si, di = (x[:].rearrange("p (two z) s -> p two z s", two=2) for x in (xT, xR))
                    for k, alu in enumerate((ALU.add, ALU.subtract)):
                        nc.vector.tensor_tensor(di[:, k], si[:, 0], si[:, 1], alu).then_inc(fly, 1)

                def rotated_lo(b):
                    for c in range(HC):
                        dve.wait_ge(xs_hi, b * HC + c + 1)
                        nc.vector.tensor_tensor(xs[:, 1, c], tp[c][:], xs[:, 0, c].bitcast(F32), ALU.subtract).then_inc(xs_lo, 1)

                def turn(b, first, final):
                    base = 2 * b * NORM_STEPS
                    for j in range(NOP):
                        delta(b, j)
                    for j in range(NOP):
                        stats(b, 0, j, d, d_done)
                    if not first:
                        butterfly(b - 1)
                    delta(b, ST - 1)
                    stats(b, 0, ST - 1, d, d_done)
                    moments_sum(nc, dve, norm_step, base, ve_done, mo)
                    for j in range(ST):
                        nc.vector.scalar_tensor_tensor(d[:, j], d[:, j], mo.mean[:, j:j + 1], gamma[:],
                                                       ALU.subtract, ALU.mult).then_inc(g_done, 1)
                    if not (first or final):
                        front_lo(b + 1)
                    moments_root(nc, dve, norm_step, base, root_done, 2 * b, mo)
                    dve.wait_ge(beta_done, b + 1)
                    at_least(dve, x1_stored, b * 16)
                    for j in range(ST):
                        dve.wait_ge(g_done, b * ST + j + 1)
                        nc.vector.scalar_tensor_tensor(x1[:, j], d[:, j], mo.inv[:, j:j + 1], xt[:, j],
                                                       ALU.mult, ALU.add).then_inc(x1_done, 1)
                    if first:
                        front_lo(b + 1)
                    for j in range(ST):
                        stats(b, 1, j, x1, x1_done)
                    if not first:
                        rotated_lo(b - 1)
                    moments_sum(nc, dve, norm_step, base + NORM_STEPS, ve_done, mo)
                    moments_root(nc, dve, norm_step, base + NORM_STEPS, root_done, 2 * b + 1, mo)
                    at_least(dve, t_done, b * HC)
                    for j in range(ST):
                        nc.vector.tensor_scalar(xn[:, j], x1[:, j], mo.mean[:, j:j + 1], mo.inv[:, j:j + 1],
                                                ALU.subtract, ALU.mult).then_inc(xn_done, 1)

                nc.vector.tensor_copy(bvb[:], bv[:].unsqueeze(2).to_broadcast([P, HC, P])).then_inc(bvb_done, 1)
                nc.vector.tensor_scalar(rs[:], rs[:], 0.0, 0.3, ALU.max, ALU.min).then_inc(rs_step, 1)
                nc.vector.tensor_scalar(su[:], su[:], 1.0 / float(np.sqrt(H)), None, ALU.mult).then_inc(rs_step, 1)
                nc.vector.tensor_scalar(wsc[:], wsc[:], 1.0 / float(np.sqrt(INTER)), None, ALU.mult).then_inc(rs_step, 1)
                dve.wait_ge(w_hi, 1)
                nc.vector.tensor_tensor(wo[:, 1], wraw, wo[:, 0].bitcast(F32), ALU.subtract).then_inc(w_lo, 1)
                front_lo(0)
                dve.wait_ge(sum_in, 16)
                nc.vector.tensor_tensor(sums[:, 0], sums[:, 0], sums[:, 1], ALU.add).then_inc(rec_step, 1)
                dve.wait_ge(rec_step, 1)
                nc.vector.reciprocal(recip[:], sums[:, 0]).then_inc(rec_step, 1)
                dve.wait_ge(bias_done, 1)
                nc.vector.tensor_tensor(bo[:], tp[0][:], bo[:], ALU.add).then_inc(rs_step, 1)
                dve.wait_ge(rs_step, 4)
                nc.vector.tensor_scalar(bo[:], bo[:], rs[:, 0:1], None, ALU.mult).then_inc(rs_step, 1)
                dve.wait_ge(rs_step, 5)
                over_batches(dve, turn)
                butterfly(B - 1)
                dve.wait_ge(ug_hi, 2)
                for i in range(2):
                    nc.vector.tensor_tensor(ugs[:, i, 1], ugr[:, i], ugs[:, i, 0].bitcast(F32), ALU.subtract).then_inc(ug_lo, 1)
                rotated_lo(B - 1)

            @block.tensor
            def _(pe):
                def transposes(b):
                    pe.wait_ge(xn_done, b * ST + ST)
                    at_least(pe, xs_lo, b * HC)
                    for c in range(HC):
                        for j in range(ST):
                            last = nc.tensor.transpose(tp[c][:, j * P:(j + 1) * P], xn[:, j, c * P:(c + 1) * P], ident[:])
                        last.then_inc(t_done, 1)

                def out_proj(b, tiles):
                    for j in tiles:
                        if j == 0:
                            pe.wait_ge(c_lo, b * HC + HC)
                            at_least(pe, d_done, b * ST)
                        if j == NOP:
                            pe.wait_ge(d_done, b * ST + 1)
                        split_product(nc, op[j % NOP][:], lambda t, c: cs[:, t, c, j * P:(j + 1) * P],
                                      lambda t, c: wo[:, t, c, :]).then_inc(o_done, 1)

                def rotation(b):
                    pe.wait_ge(fly, b * 2 + 2)
                    for c in range(HC):
                        pair = c // 2 * 2
                        nc.tensor.matmul(tp[c][:], had[:, 0], xR[:, pair], start=True, stop=False)
                        nc.tensor.matmul(tp[c][:], had[:, c % 2], xR[:, pair + 1], start=False, stop=True).then_inc(rot_done, 1)

                def down(b, chunks):
                    for i in chunks:
                        pe.wait_ge(wdf_done, b * WC + i)
                        nc.tensor.matmul(wp[:], had[:, 0], wd[:, i], start=True, stop=True).then_inc(wrot_done, 1)

                def turn(b, first, final):
                    if not first:
                        transposes(b - 1)
                    out_proj(b, (ST - 1,))
                    pe.wait_ge(wd_in, b * 32 + 32)
                    down(b, range(WC // 2))
                    if not first:
                        rotation(b - 1)
                    down(b, range(WC // 2, WC))
                    if not final:
                        out_proj(b + 1, range(NOP))

                pe.wait_ge(bvb_done, 1)
                for c in range(HC):
                    last = nc.tensor.matmul(tp[0][:], bvb[:, c], wraw[:, c], start=c == 0, stop=c == HC - 1)
                last.then_inc(bias_done, 1)
                pe.wait_ge(w_lo, 1)
                out_proj(0, range(NOP))
                pe.wait_ge(rs_step, 4)
                pe.wait_ge(had_done, 1)
                over_batches(pe, turn)
                transposes(B - 1)
                rotation(B - 1)


def ffn(nc, io, scr, out, early, hand):
    GR = INTER // (GC * P)
    UN = B * GC
    with ExitStack() as stack:
        m = Mem(nc, stack, "ff")
        ORDER = [B - 1] + list(range(B - 1))
        xs = [hand.xs] + [m.sb(f"xs{i}", [P, 2, HC, S], F32R) for i in range(1, B)]
        x1 = [hand.x1, early.ca, early.cb, early.rb]
        ugr = hand.ugr
        ugs = [hand.ugs0, m.sb("ugs1", [P, 2, 2, HC, GC * P], F32R)]
        wds = [m.sb(f"wds{i}", [P, GC, 2, H], F32R) for i in range(2)]
        scale = [m.sb(f"scale{i}", [P, 2, GC]) for i in range(2)]
        silu = [m.sb(f"silu{i}", [P, S]) for i in range(2)]
        hf = [m.sb(f"hf{i}", [P, S]) for i in range(2)]
        hs = [m.sb(f"hs{i}", [P, 2, S], F32R) for i in range(2)]
        up = [m.ps(f"up{i}", [P, S]) for i in range(2)]
        gp = [m.ps(f"gp{i}", [P, S]) for i in range(2)]
        yp = [m.ps(f"yp{i}", [P, H]) for i in range(ST)]

        (ug_in, ug_hi, ug_lo, gate_done, silu_done, hf_done, h_hi, h_lo, down_done,
         y_read, out_stored) = (m.sem(n) for n in (
             "ug_in", "ug_hi", "ug_lo", "gate_done", "silu_done", "hf_done", "h_hi",
             "h_lo", "down_done", "y_read", "out_stored"))
        xs_in, x1_in = m.sems("xs_in", B), m.sems("x1_in", B)
        wd_in = m.sems("wd_in", 2)
        assert GR % 2 == 0 and GR >= 6

        def in_pairs(eng, group):
            for k in range(2):
                group(k, k, False)
            with eng.Fori(1, GR // 2 - 1) as i:
                for k in range(2):
                    group(i * 2 + k, k, False)
            for k in range(2):
                group(GR - 2 + k, k, k == 1)

        with nc.Block() as block:
            @block.sync
            def _(sp):
                def load_down(g, k):
                    at_least(sp, down_done, (g - 1) * UN)
                    sp.dma_start(wds[k][:].bitcast(F32), scr["wd"][:, bass.ds(g * GC, GC)]).then_inc(wd_in[k], 16)
                    sp.dma_start(scale[k][:], io["ws_ug"][:, :, bass.ds(g * GC, GC)]).then_inc(wd_in[k], 16)

                def load_rotated(b):
                    sp.dma_start(xs[b][:].bitcast(F32), scr["xs"][ORDER[b]].rearrange("t p c s -> p t c s")).then_inc(xs_in[b], 16)

                def load_rows(b):
                    sp.dma_start(x1[b], scr["x1"][ORDER[b]]).then_inc(x1_in[b], 16)

                load_down(0, 0)
                load_up_gate(sp, io, ugr, 1, ug_in)
                load_rotated(1)
                load_rows(1)
                for b in range(2, B):
                    load_rotated(b)
                    load_rows(b)
                load_down(1, 1)
                with sp.Fori(1, GR // 2) as i:
                    for k in range(2):
                        g = i * 2 + k
                        sp.wait_ge(ug_lo, (g - 1) * 2)
                        load_up_gate(sp, io, ugr, g, ug_in)
                        load_down(g, k)
                for b in range(B):
                    for j in range(ST):
                        sp.wait_ge(y_read, ((GR - 1) * B + b) * ST + j + 1)
                        sp.dma_start(out[ORDER[b], j * P:(j + 1) * P], x1[b][:, j]).then_inc(out_stored, 16)
                sp.wait_ge(out_stored, B * ST * 16)

            @block.scalar
            def _(act):
                def split_weights(g, k):
                    act.wait_ge(ug_in, g * 32)
                    at_least(act, gate_done, (g - 1) * UN)
                    for i in range(2):
                        nc.scalar.activation(ugs[k][:, i, 0], ugr[:, i], ACT.Copy).then_inc(ug_hi, 1)

                def group(g, k, final):
                    act.wait_ge(wd_in[k], (g - k) * 16 + 32)
                    for u in range(UN):
                        n = g * UN + u
                        if u == 2 and not final:
                            split_weights(g + 1, 1 - k)
                        act.wait_ge(gate_done, n + 1)
                        at_least(act, hf_done, n - 1)
                        nc.scalar.activation(silu[u % 2][:], gp[u % 2][:], ACT.Silu,
                                             scale=scale[k][:, 1, u % GC:u % GC + 1]).then_inc(silu_done, 1)
                        act.wait_ge(hf_done, n + 1)
                        at_least(act, down_done, n - 1)
                        nc.scalar.activation(hs[u % 2][:, 0], hf[u % 2][:], ACT.Copy).then_inc(h_hi, 1)

                in_pairs(act, group)

            @block.vector
            def _(dve):
                def split_weights(g, k):
                    dve.wait_ge(ug_hi, g * 2)
                    for i in range(2):
                        nc.vector.tensor_tensor(ugs[k][:, i, 1], ugr[:, i], ugs[k][:, i, 0].bitcast(F32),
                                                ALU.subtract).then_inc(ug_lo, 1)

                def accumulate(g, b):
                    dve.wait_ge(down_done, (g * B + b + 1) * GC)
                    if isinstance(g, int) and g == 0:
                        if b:
                            dve.wait_ge(x1_in[b], 16)
                    else:
                        dve.wait_ge(y_read, ((g - 1) * B + b + 1) * ST)
                    for j in range(ST):
                        nc.vector.tensor_tensor(x1[b][:, j], yp[j][:], x1[b][:, j], ALU.add).then_inc(y_read, 1)

                def group(g, k, final):
                    dve.wait_ge(wd_in[k], (g - k) * 16 + 32)
                    for u in range(UN):
                        n = g * UN + u
                        if u == 2 and not final:
                            split_weights(g + 1, 1 - k)
                        dve.wait_ge(silu_done, n + 1)
                        at_least(dve, h_hi, n - 1)
                        nc.vector.scalar_tensor_tensor(hf[u % 2][:], up[u % 2][:], scale[k][:, 0, u % GC:u % GC + 1],
                                                       silu[u % 2][:], ALU.mult, ALU.mult).then_inc(hf_done, 1)
                        dve.wait_ge(h_hi, n + 1)
                        nc.vector.tensor_tensor(hs[u % 2][:, 1], hf[u % 2][:], hs[u % 2][:, 0].bitcast(F32),
                                                ALU.subtract).then_inc(h_lo, 1)
                        if u % GC == 0:
                            if u:
                                accumulate(g, u // GC - 1)
                            elif not (isinstance(g, int) and g == 0):
                                accumulate(g - 1, B - 1)

                in_pairs(dve, group)
                accumulate(GR - 1, B - 1)

            @block.tensor
            def _(pe):
                def gate_up(g, k, u):
                    b, i = u // GC, u % GC
                    if isinstance(g, int) and g == 0 and i == 0 and b:
                        pe.wait_ge(xs_in[b], 16)
                    if u == 0:
                        at_least(pe, ug_lo, g * 2)
                    at_least(pe, hf_done, g * UN + u - 1)
                    for w, acc in ((0, up), (1, gp)):
                        last = split_product(nc, acc[u % 2][:], lambda t, c: ugs[k][:, w, t, c, i * P:(i + 1) * P],
                                             lambda t, c: xs[b][:, t, c])
                    last.then_inc(gate_done, 1)

                def down(g, k, u):
                    b, i = u // GC, u % GC
                    if u == 0:
                        pe.wait_ge(wd_in[k], (g - k) * 16 + 32)
                    if i == 0:
                        at_least(pe, y_read, (g * B + b) * ST)
                    pe.wait_ge(h_lo, g * UN + u + 1)
                    for j in range(ST):
                        last = split_product(nc, yp[j][:], lambda t, c: hs[u % 2][:, t, j * P:(j + 1) * P],
                                             lambda t, c: wds[k][:, i, t], chunks=1, first=i == 0, final=i == GC - 1)
                    last.then_inc(down_done, 1)

                def group(g, k, final):
                    for u in range(UN):
                        if u + 1 < UN:
                            gate_up(g, k, u + 1)
                        elif not final:
                            gate_up(g + 1, 1 - k, 0)
                        down(g, k, u)

                gate_up(0, 0, 0)
                in_pairs(pe, group)


def build(nc, io, out):
    def scratch(name, shape, dt=F32):
        return nc.dram_tensor(f"scr_{name}", shape, dt).ap()

    scr = {
        "q": scratch("q", [2, B, H, S]),
        "k": scratch("k", [2, B, H, TE]),
        "v": scratch("v", [B, NH, P, TT, 2 * HD + 2]),
        "c": scratch("c", [2, B, H, S]),
        "sum": scratch("sum", [2, B * NH * S]),
        "rec": scratch("rec", [B, NH, S]),
        "x1": scratch("x1", [B, P, ST, H]),
        "xs": scratch("xs", [B, 2, P, HC, S]),
        "wdb": scratch("wdb", [P, INTER // P, H]),
        "wd": scratch("wd", [P, INTER // P, 2, H]),
    }
    for name in ("q", "k", "c"):
        scr[name + "4"] = scr[name].rearrange("z b (h d) s -> z (b h) d s", d=HD)
    scr["v4"] = scr["v"].rearrange("b h p t w -> (b h) p t w")
    scr["sum4"] = scr["sum"].rearrange("z (h s) -> z h s", s=S)
    prepare(nc, io, scr)
    with ExitStack() as stack:
        early = Early(Mem(nc, stack, "early"))
        attention(nc, io, scr, early)
        hand = Handover(Mem(nc, stack, "hand"))
        project(nc, io, scr, early, hand)
        ffn(nc, io, scr, out, early, hand)


def hadamard(n):
    h = np.ones((1, 1), np.float32)
    while h.shape[0] < n:
        h = np.block([[h, h], [h, -h]])
    return np.ascontiguousarray(h.astype(np.float32))


def kernel(**inputs):
    import concourse.bacc as bacc
    from concourse.bass_utils import run_bass_kernel_spmd

    a = {k: np.asarray(v) for k, v in inputs.items()}
    def columns(v):
        return v.reshape(-1, P).T

    arrays = {
        "x": a["x"],
        "ctxT": a["ctx_2048"].transpose(0, 2, 1),
        "mask": a["mask_BxS2_ik0"],
        "bq": columns(a["L0_xattn_bq"]), "bk": columns(a["L0_xattn_bk"]), "bv": columns(a["L0_xattn_bv"]),
        "bo": a["L0_xattn_bo"],
        "wqT": a["L0_xattn_Wq"].T, "wkT": a["L0_xattn_Wk"].T, "wvT": a["L0_xattn_Wv"].T, "woT": a["L0_xattn_Wo"].T,
        "gamma": a["L0_xattn_ln_gamma"], "beta": a["L0_xattn_ln_beta"],
        "rs": a["L0_xattn_residual_scale"].reshape(1),
        "su_ug": columns(a["L0_ffn_SU_ug"]), "su_dp": columns(a["L0_ffn_SU_dp"]),
        "ws_ug": columns(a["L0_ffn_Wscale_ug"]).reshape(P, 2, INTER // P), "ws_dp": a["L0_ffn_Wscale_dp"],
        "upT": a["L0_ffn_W_up"].T, "gateT": a["L0_ffn_W_gate"].T, "wdT": a["L0_ffn_W_down"].T,
        "ident": np.eye(P, dtype=np.float32), "had": hadamard(P),
    }
    arrays = {f"in_{k}": np.ascontiguousarray(v) for k, v in arrays.items()}
    nc = bacc.Bacc("TRN2", target_bir_lowering=False, num_devices=1)
    io = {k[3:]: nc.dram_tensor(k, v.shape, mybir.dt.from_np(v.dtype), kind="ExternalInput").ap()
          for k, v in arrays.items()}
    out = nc.dram_tensor("out", (B, S, H), F32, kind="ExternalOutput").ap()
    build(nc, io, out)
    r = run_bass_kernel_spmd(nc, [arrays], core_ids=[0])
    return r.results[0]["out"]
```
